# Optimizing a Trainium2 kernel written in Bass

```python
import numpy as np
import jax
import jax.numpy as jnp

def _softmax(x, axis=-1):
    return jax.nn.softmax(x, axis=axis)

def _gelu(x):
    return jax.nn.gelu(x, approximate=True)

def _silu(x):
    return jax.nn.silu(x)

def _sigmoid(x):
    return jax.nn.sigmoid(x)

def _layernorm(x, axis=-1, eps=1e-05):
    m = jnp.mean(x, axis=axis, keepdims=True)
    v = jnp.var(x, axis=axis, keepdims=True)
    return (x - m) / jnp.sqrt(v + eps)

def _scatter_add(tgt, idx, src, axis=0):
    return tgt.at[idx].add(src)

def _segment_sum(src, seg, n):
    return jax.ops.segment_sum(src, seg, n)
kernel_name = 'mk_adj_ffn_d1_adj_r2_74424a'

def setup_inputs(seed: int=0):
    np.random.seed(seed)
    _w = jnp.asarray

    def _rec_inputs():
        import jax
        import jax.numpy as jnp
        _gk = jax.random.key(seed)
        x = -0.0002928 + 1 * jax.random.normal(jax.random.fold_in(_gk, 1), (128, 128, 128), jnp.float32)
        _a = jax.random.bernoulli(jax.random.fold_in(_gk, 2), 0.125, (128, 128))
        _a = jnp.logical_or(_a, jnp.eye(128, dtype=bool))
        _af = _a.astype(jnp.float32)
        adj = _af
        return (x, adj)
    x, adj = _rec_inputs()

    def _L0_gnn_setup():
        import jax, jax.numpy as jnp
        import numpy as np
        ALPHA = 0.2
        key = jax.random.key(seed)
        k1, k2, k3, k4 = jax.random.split(key, 4)
        B, N, Fin, Fout = (8, 1024, 128, 128)
        h = jax.random.normal(k1, (B, N, Fin), dtype=jnp.float32)
        adj = jax.random.randint(k2, (N, N), 0, 2).astype(jnp.float32)
        adj = jnp.maximum(adj, jnp.eye(N, dtype=jnp.float32))

        def xavier(k, shape, gain=1.414):
            fan_in, fan_out = (shape[0], shape[1])
            a = gain * np.sqrt(6.0 / (fan_in + fan_out))
            return jax.random.uniform(k, shape, dtype=jnp.float32, minval=-a, maxval=a)
        W = xavier(k3, (Fin, Fout))
        a = xavier(k4, (2 * Fout, 1))
        return {'h': h, 'adj_matrix': adj, 'W': W, 'a': a}
    _L0_gnn_all = _L0_gnn_setup()
    _L0_gnn_in = {k: v for k, v in _L0_gnn_all.items() if k in ('W', 'a')}
    del _L0_gnn_all

    def _L0_ffn_setup():
        import jax, jax.numpy as jnp
        import numpy as np
        TOP_K = 2
        LN_EPS = 1e-05
        key = jax.random.key(seed)
        ks = jax.random.split(key, 8)
        B, S, D, E, H = (16, 512, 128, 8, 512)
        x = jax.random.normal(ks[0], (B, S, D), dtype=jnp.float32)
        Wr = jax.random.normal(ks[1], (D, E), dtype=jnp.float32) * 0.1
        br = jnp.zeros((E,), dtype=jnp.float32)
        ln_g = jnp.ones((E, D), dtype=jnp.float32)
        ln_b = jnp.zeros((E, D), dtype=jnp.float32)
        W1 = jax.random.normal(ks[2], (E, D, H), dtype=jnp.float32) * (1.0 / np.sqrt(D))
        b1 = jnp.zeros((E, H), dtype=jnp.float32)
        W2 = jax.random.normal(ks[3], (E, H, D), dtype=jnp.float32) * (1.0 / np.sqrt(H))
        b2 = jnp.zeros((E, D), dtype=jnp.float32)
        return {'x': x, 'Wr': Wr, 'br': br, 'ln_g': ln_g, 'ln_b': ln_b, 'W1': W1, 'b1': b1, 'W2': W2, 'b2': b2}
    _L0_ffn_all = _L0_ffn_setup()
    _L0_ffn_in = {k: v for k, v in _L0_ffn_all.items() if k in ('Wr', 'br', 'ln_g', 'ln_b', 'W1', 'b1', 'W2', 'b2')}
    del _L0_ffn_all
    return {'x': x, 'adj': adj, 'L0_gnn_W': _L0_gnn_in['W'], 'L0_gnn_a': _L0_gnn_in['a'], 'L0_ffn_Wr': _L0_ffn_in['Wr'], 'L0_ffn_br': _L0_ffn_in['br'], 'L0_ffn_ln_g': _L0_ffn_in['ln_g'], 'L0_ffn_ln_b': _L0_ffn_in['ln_b'], 'L0_ffn_W1': _L0_ffn_in['W1'], 'L0_ffn_b1': _L0_ffn_in['b1'], 'L0_ffn_W2': _L0_ffn_in['W2'], 'L0_ffn_b2': _L0_ffn_in['b2']}

def reference(x, adj, L0_gnn_W, L0_gnn_a, L0_ffn_Wr, L0_ffn_br, L0_ffn_ln_g, L0_ffn_ln_b, L0_ffn_W1, L0_ffn_b1, L0_ffn_W2, L0_ffn_b2):
    import jax
    import jax.numpy as jnp

    def _L0_gnn_ref(h, adj_matrix, W, a):
        import jax, jax.numpy as jnp
        import numpy as np
        ALPHA = 0.2
        Fout = W.shape[1]
        Wh = jnp.einsum('bnf,fo->bno', h, W)
        a1, a2 = (a[:Fout, 0], a[Fout:, 0])
        s1 = Wh @ a1
        s2 = Wh @ a2
        e = s1[:, :, None] + s2[:, None, :]
        e = jnp.where(e >= 0, e, ALPHA * e)
        e = jnp.where(adj_matrix[None] == 0, -jnp.inf, e)
        attention = jax.nn.softmax(e, axis=-1)
        h_prime = jnp.einsum('bij,bjo->bio', attention, Wh)
        return h_prime

    def _L0_ffn_ref(x, Wr, br, ln_g, ln_b, W1, b1, W2, b2):
        import jax, jax.numpy as jnp
        import numpy as np
        TOP_K = 2
        LN_EPS = 1e-05
        B, S, D = x.shape
        N = B * S
        xt = x.reshape(N, D)
        logits = xt @ Wr + br
        probs = jax.nn.softmax(logits, axis=-1)
        top_p, top_idx = jax.lax.top_k(probs, TOP_K)
        weights = top_p / top_p.sum(axis=-1, keepdims=True)
        mu = xt.mean(axis=-1, keepdims=True)
        var = ((xt - mu) ** 2).mean(axis=-1, keepdims=True)
        xn = (xt - mu) * jax.lax.rsqrt(var + LN_EPS)
        xe = xn[None, :, :] * ln_g[:, None, :] + ln_b[:, None, :]
        h = jax.nn.gelu(jnp.einsum('end,edh->enh', xe, W1) + b1[:, None, :], approximate=False)
        y = jnp.einsum('enh,ehd->end', h, W2) + b2[:, None, :]
        y_tok = jnp.transpose(y, (1, 0, 2))
        sel = jnp.take_along_axis(y_tok, top_idx[:, :, None], axis=1)
        out = (weights[:, :, None] * sel).sum(axis=1)
        return out.reshape(B, S, D)
    x = x + _L0_gnn_ref(_layernorm(x, axis=-1), adj, L0_gnn_W, L0_gnn_a)
    x = x + _L0_ffn_ref(_layernorm(x, axis=-1), L0_ffn_Wr, L0_ffn_br, L0_ffn_ln_g, L0_ffn_ln_b, L0_ffn_W1, L0_ffn_b1, L0_ffn_W2, L0_ffn_b2)
    return x

_drawn_inputs = setup_inputs


def setup_inputs(seed=0):
    import zlib

    import numpy as np

    out = dict(_drawn_inputs(seed))
    spreads = {'L0_ffn_br': (0.0, 0.1),
     'L0_ffn_ln_g': (1.0, 0.2),
     'L0_ffn_ln_b': (0.0, 0.1),
     'L0_ffn_b1': (0.0, 0.1),
     'L0_ffn_b2': (0.0, 0.1)}
    factors = {}
    for name, (base, spread) in spreads.items():
        noise = np.random.default_rng([zlib.crc32(name.encode()), seed]).standard_normal(out[name].shape)
        drawn = base * np.exp(spread * noise) if base else spread * noise
        out[name] = jnp.asarray(drawn.astype(out[name].dtype))
    for name, factor in factors.items():
        out[name] = (out[name] * factor).astype(out[name].dtype)
    return out
```

```python
from contextlib import ExitStack

import concourse.bass as bass
from concourse import mybir

F32 = mybir.dt.float32
F32R = mybir.dt.float32r
BF16 = mybir.dt.bfloat16
I32 = mybir.dt.int32
ALU = mybir.AluOpType
ACT = mybir.ActivationFunctionType
AX = mybir.AxisListType

P = 128
OCT = 8
HALF = OCT // 2
TILE = 512
CH = TILE // P
EPS = 1e-5
SLOPE = 0.2
MASKED = -1e30
LOWEST = -3e38


def moe_kernel(nc, x, adj, gnn_w, gnn_a, wr, br, ln_g, ln_b, w1, b1, w2, b2, out):
    G, N, D = x.shape
    E, _, H = w1.shape
    HC = H // P
    NO = G // OCT
    TOKENS = G * N
    ROWS = 2 * TOKENS
    NT = ROWS // TILE + E - 1
    DEAD = E - 1
    CAP = TOKENS + TILE
    R = D + 2
    assert N == P and D == P and G % OCT == 0 and H % P == 0 and ROWS % TILE == 0

    rows_dram = nc.dram_tensor("expert_rows", [E * CAP + DEAD * TILE, R], F32).ap()
    pads_dram = nc.dram_tensor("pad_rows", [E * TILE, R], F32).ap()
    y_dram = nc.dram_tensor("expert_out", [ROWS + (E + DEAD) * TILE, D], F32).ap()

    def wait_apart(engine, sem, value, passed):
        engine.wait_ge(sem, value)
        if not isinstance(value, int):
            engine.sem_inc(passed, 1)

    def ds(start, size):
        return slice(start, start + size) if isinstance(start, int) else bass.ds(start, size)

    with ExitStack() as whole:
        def keep(name, shape, dt=F32):
            return whole.enter_context(nc.sbuf_tensor(name, shape, dt))

        tok = keep("tok", [P, G, D])
        w1s = keep("w1s", [P, E, 2, H], F32R)
        w2s = keep("w2s", [P, E, 2, HC * D], F32R)
        bias = keep("bias", [P, E, HC + 1])
        ident = keep("ident", [P, P])
        table = keep("table", [1, 3, NT], I32)

        before_experts = whole.enter_context(ExitStack())

        def keep_to_plan(name, shape, dt=F32):
            return before_experts.enter_context(nc.sbuf_tensor(name, shape, dt))

        tri = keep_to_plan("tri", [P, P], BF16)
        ones = keep_to_plan("ones", [P, P], BF16)
        gw = keep_to_plan("gw", [P, D])
        a1rep = keep_to_plan("a1rep", [P, P])
        a2rep = keep_to_plan("a2rep", [P, P])
        mask = keep_to_plan("mask", [P, P])
        wrs = keep_to_plan("wrs", [P, E])
        brs = keep_to_plan("brs", [P, E])
        ranked = keep_to_plan("ranked", [P, E])
        region = keep_to_plan("region", [P, E])
        ids = keep_to_plan("ids", [P, 2, G], I32)
        taken = keep_to_plan("taken", [P, E], BF16)
        tails = keep_to_plan("tails", [1, E], I32)

        with ExitStack() as ctx:
            def sb(name, shape, dt=F32):
                return ctx.enter_context(nc.sbuf_tensor(name, shape, dt))

            def sem(name):
                return ctx.enter_context(nc.semaphore(name))

            w1raw = sb("w1raw", [P, E, H])
            w2raw = sb("w2raw", [P, E, HC * D])
            w1g = sb("w1g", [P, 2, H])
            adjs = sb("adjs", [P, P])
            arow = sb("arow", [P, 2, D])
            prod = sb("prod", [P, D])
            acol = sb("acol", [P, 2])
            NV = E * HC + 3 * E
            vecs = sb("vecs", [NV, P])
            cols = sb("cols", [P, NV])
            pads = sb("pads", [P, E + DEAD, CH, R])
            ps_cols = ctx.enter_context(nc.psum_tensor("ps_cols", [P, NV], F32))
            ps_b1 = ctx.enter_context(nc.psum_tensor("ps_b1", [P, E * HC], F32))
            B2, LG, LB = E * HC, E * HC + E, E * HC + 2 * E

            small_in = sem("small_in")
            tok_in = sem("tok_in")
            w1_in = sem("w1_in")
            w2_in = sem("w2_in")
            fills = sem("fills")
            ident_ok = sem("ident_ok")
            iotas = sem("iotas")
            pads_zero = sem("pads_zero")
            pads_ok = sem("pads_ok")
            pads_out = sem("pads_out")
            cols_ps = sem("cols_ps")
            cols_ok = sem("cols_ok")
            b1_ps = sem("b1_ps")
            bias_ok = sem("bias_ok")
            scaled = sem("scaled")
            high1 = sem("high1")
            low1 = sem("low1")
            high2 = sem("high2")
            low2 = sem("low2")
            acols = sem("acols")
            arep = sem("arep")
            step = sem("step")

            with nc.Block() as block:
                @block.sync
                def _(sp):
                    sp.dma_start(vecs[0:B2, :], b1.rearrange("e (c p) -> (e c) p", p=P)).then_inc(small_in, 16)
                    sp.dma_start(vecs[B2:LG, :], b2).then_inc(small_in, 16)
                    sp.dma_start(vecs[LG:LB, :], ln_g).then_inc(small_in, 16)
                    sp.dma_start(vecs[LB:NV, :], ln_b).then_inc(small_in, 16)
                    sp.dma_start(gw[:], gnn_w).then_inc(small_in, 16)
                    sp.dma_start(adjs[:], adj).then_inc(small_in, 16)
                    sp.dma_start(wrs[:], wr).then_inc(small_in, 16)
                    sp.dma_start(brs[:], br.partition_broadcast(P)).then_inc(small_in, 16)
                    for k in range(2):
                        a_k = gnn_a[k * D:(k + 1) * D, :].rearrange("d o -> (d o)")
                        sp.dma_start(arow[:, k, :], a_k.partition_broadcast(P)).then_inc(small_in, 16)
                    sp.dma_start(w1raw[:], w1.rearrange("e d h -> d e h")).then_inc(w1_in, 16)
                    sp.dma_start(w2raw[:].rearrange("p e (c d) -> p e c d", d=D),
                                 w2.rearrange("e (c p) d -> p e c d", p=P)).then_inc(w2_in, 16)
                    for n in range(4):
                        g0, g1 = n * G // 4, (n + 1) * G // 4
                        sp.dma_start(tok[:, g0:g1, :], x[g0:g1].rearrange("g p d -> p g d")).then_inc(tok_in, 16)
                    sp.wait_ge(pads_ok, 1)
                    sp.dma_start(pads_dram.rearrange("(e c p) r -> p e c r", p=P, c=CH),
                                 pads[:, 0:E]).then_inc(pads_out, 16)
                    sp.dma_start(rows_dram[E * CAP:, :].rearrange("(e c p) r -> p e c r", p=P, c=CH),
                                 pads[:, E:]).then_inc(pads_out, 16)
                    sp.wait_ge(pads_out, 32)
                    sp.wait_ge(tok_in, 64)

                @block.gpsimd
                def _(pool):
                    nc.gpsimd.memset(ident[:], 0.0).then_inc(fills, 1)
                    nc.gpsimd.memset(tri[:], 1.0).then_inc(fills, 1)
                    pool.wait_ge(fills, 2)
                    nc.gpsimd.affine_select(out=ident[:], in_=ident[:], compare_op=ALU.not_equal, fill=1.0, base=0,
                                            pattern=[[-1, P]], channel_multiplier=1).then_inc(ident_ok, 1)
                    nc.gpsimd.affine_select(out=tri[:], in_=tri[:], compare_op=ALU.is_gt, fill=0.0, base=0,
                                            pattern=[[1, P]], channel_multiplier=-1).then_inc(iotas, 1)
                    nc.gpsimd.iota(ids[:], pattern=[[1, 2], [2 * N, G]], base=0, channel_multiplier=2).then_inc(iotas, 1)
                    nc.gpsimd.iota(ranked[:], pattern=[[-1, E]], base=E, channel_multiplier=0,
                                   allow_small_or_imprecise_dtypes=True).then_inc(iotas, 1)
                    nc.gpsimd.iota(region[:], pattern=[[CAP, E]], base=0, channel_multiplier=0,
                                   allow_small_or_imprecise_dtypes=True).then_inc(iotas, 1)
                    nc.gpsimd.memset(pads[:], 0.0).then_inc(pads_zero, 1)
                    pool.wait_ge(pads_zero, 1)
                    nc.gpsimd.iota(pads[:, :, :, D:D + 1].bitcast(I32),
                                   pattern=[[TILE, E + DEAD], [P, CH], [1, 1]], base=ROWS,
                                   channel_multiplier=1).then_inc(pads_ok, 1)
                    pool.wait_ge(iotas, 4)

                @block.tensor
                def _(pe):
                    pe.wait_ge(small_in, 160)
                    pe.wait_ge(ident_ok, 1)
                    nc.tensor.transpose(ps_cols[:], vecs[:], ident[0:NV, 0:NV]).then_inc(cols_ps, 1)
                    pe.wait_ge(cols_ok, 1)
                    pe.wait_ge(w1_in, 16)
                    for e in range(E):
                        for c in range(HC):
                            mm = nc.tensor.matmul(ps_b1[:, e * HC + c:e * HC + c + 1], w1raw[:, e, c * P:(c + 1) * P],
                                                  cols[:, LB + e:LB + e + 1], start=True, stop=True)
                    mm.then_inc(b1_ps, 1)

                @block.scalar
                def _(act):
                    act.wait_ge(cols_ok, 1)
                    act.wait_ge(w1_in, 16)
                    for e in range(E):
                        if e >= 2:
                            act.wait_ge(low1, e - 1)
                        nc.scalar.activation(w1g[:, e % 2, :], w1raw[:, e, :], ACT.Copy,
                                             scale=cols[:, LG + e:LG + e + 1]).then_inc(scaled, 1)
                        act.wait_ge(scaled, e + 1)
                        nc.scalar.activation(w1s[:, e, 0, :], w1g[:, e % 2, :], ACT.Copy).then_inc(high1, 1)
                    act.wait_ge(w2_in, 16)
                    for e in range(E):
                        nc.scalar.activation(w2s[:, e, 0, :], w2raw[:, e, :], ACT.Copy).then_inc(high2, 1)

                @block.vector
                def _(dve):
                    steps = [0]

                    def link(ins):
                        steps[0] += 1
                        ins.then_inc(step, 1)
                        dve.wait_ge(step, steps[0])

                    nc.vector.memset(ones[:], 1.0)
                    nc.vector.memset(taken[:], 0.0)
                    dve.wait_ge(small_in, 160)
                    link(nc.vector.tensor_scalar(mask[:], adjs[:], 0.0, MASKED, ALU.is_equal, ALU.mult))
                    for k, rep in enumerate((a1rep, a2rep)):
                        link(nc.vector.tensor_tensor_reduce(out=prod[:], in0=gw[:], in1=arow[:, k, :], scale=1.0,
                                                            scalar=0.0, op0=ALU.mult, op1=ALU.add,
                                                            accum_out=acol[:, k:k + 1]))
                        link(nc.vector.tensor_copy(rep[:], acol[:, k:k + 1].to_broadcast([P, P])))
                    dve.wait_ge(cols_ps, 1)
                    nc.vector.tensor_copy(cols[:], ps_cols[:]).then_inc(cols_ok, 1)
                    dve.wait_ge(cols_ok, 1)
                    nc.vector.tensor_copy(bias[:, :, HC:HC + 1], cols[:, B2:LG].unsqueeze(2)).then_inc(bias_ok, 1)
                    dve.wait_ge(b1_ps, 1)
                    nc.vector.tensor_tensor(bias[:, :, 0:HC], ps_b1[:].rearrange("p (e c) -> p e c", c=HC),
                                            cols[:, 0:B2].rearrange("p (e c) -> p e c", c=HC),
                                            ALU.add).then_inc(bias_ok, 1)
                    for e in range(E):
                        dve.wait_ge(high1, e + 1)
                        nc.vector.tensor_tensor(w1s[:, e, 1, :], w1g[:, e % 2, :], w1s[:, e, 0, :].bitcast(F32),
                                                ALU.subtract).then_inc(low1, 1)
                    for e in range(E):
                        dve.wait_ge(high2, e + 1)
                        nc.vector.tensor_tensor(w2s[:, e, 1, :], w2raw[:, e, :], w2s[:, e, 0, :].bitcast(F32),
                                                ALU.subtract).then_inc(low2, 1)
                    dve.wait_ge(low2, E)
                    dve.wait_ge(bias_ok, 2)

        with ExitStack() as ctx:
            def sb(name, shape, dt=F32):
                return ctx.enter_context(nc.sbuf_tensor(name, shape, dt))

            def ps(name, shape):
                return ctx.enter_context(nc.psum_tensor(name, shape, F32))

            def sem(name):
                return ctx.enter_context(nc.semaphore(name))

            xn = sb("xn", [P, OCT, D])
            xnT = sb("xnT", [P, OCT, P])
            wh = sb("wh", [P, OCT, D])
            um = sb("um", [P, OCT, P])
            ex = sb("ex", [P, OCT, P])
            prT = sb("prT", [P, OCT, P])
            xhT = sb("xhT", [P, OCT, P])
            stage = [sb(f"stage{r}", [P, 2, OCT, R]) for r in range(2)]
            slots = [sb(f"slots{r}", [P, 2, OCT], I32) for r in range(2)]
            bn = sb("bn", [P, OCT, 6])
            mv = sb("mv", [P, OCT, 2])
            var1 = sb("var1", [P, OCT])
            seed1 = sb("seed1", [P, OCT])
            root1 = sb("root1", [P, OCT])
            bn2 = sb("bn2", [P, OCT, 6])
            mv2 = sb("mv2", [P, OCT, 2])
            var2 = sb("var2", [P, 2, OCT])
            seed2 = sb("seed2", [P, 2, OCT])
            root2 = sb("root2", [P, 2, OCT])
            tiny = sb("tiny", [P, 2, OCT])
            ratio = sb("ratio", [P, OCT])
            top = sb("top", [P, OCT])
            ntop = sb("ntop", [P, OCT])
            nbig = sb("nbig", [P, OCT])
            den = sb("den", [P, OCT])
            rden = sb("rden", [P, OCT])
            lg = sb("lg", [P, OCT, E])
            lg2 = sb("lg2", [P, OCT, E])
            eq = sb("eq", [P, OCT, E])
            hot = sb("hot", [P, 2, OCT, E])
            best = sb("best", [P, 2, OCT])
            pick = sb("pick", [P, OCT])
            both = sb("both", [P, OCT, E], BF16)
            place = sb("place", [P, OCT, E])
            chosen = sb("chosen", [P, 2, OCT, E])
            gap = sb("gap", [P, OCT])
            egap = sb("egap", [P, OCT])
            share = sb("share", [P, OCT])
            new = sb("new", [P, E])

            ps_t = [ps(f"ps_t{h}", [P, HALF, P]) for h in range(2)]
            ps_wh = ps("ps_wh", [P, HALF, D])
            ps_u = [ps(f"ps_u{h}", [P, HALF, P]) for h in range(2)]
            ps_h = [ps(f"ps_h{h}", [P, HALF, D]) for h in range(2)]
            ps_m = ps("ps_m", [P, 2, OCT * E])

            var1_ok = sem("var1_ok")
            ln1_ok = sem("ln1_ok")
            seed1_ok = sem("seed1_ok")
            xn_ok = sem("xn_ok")
            xnT_ps = sem("xnT_ps")
            xnT_ok = sem("xnT_ok")
            wh_ps = sem("wh_ps")
            wh_ok = sem("wh_ok")
            u_ps = sem("u_ps")
            u_read = sem("u_read")
            e_ok = sem("e_ok")
            ex_ok = sem("ex_ok")
            prT_ps = sem("prT_ps")
            prT_ok = sem("prT_ok")
            h_ps = sem("h_ps")
            h_read = sem("h_read")
            var2_ok = sem("var2_ok")
            ln2_ok = sem("ln2_ok")
            seed2_ok = sem("seed2_ok")
            xh_ok = sem("xh_ok")
            copied = sem("copied")
            passed_dve = sem("passed_dve")
            passed_pool = sem("passed_pool")
            xhT_ps = sem("xhT_ps")
            xhT_ok = sem("xhT_ok")
            lg_ps = sem("lg_ps")
            lg_read = sem("lg_read")
            gap_ok = sem("gap_ok")
            egap_ok = sem("egap_ok")
            both_ok = sem("both_ok")
            rank_ps = sem("rank_ps")
            slots_ok = sem("slots_ok")
            scattered = [sem(f"scattered{r}") for r in range(2)]
            step = sem("step")

            def half(h):
                return slice(h * HALF, (h + 1) * HALF)


            def pe_front(pe, i, fresh):
                for h in range(2):
                    pe.wait_ge(xn_ok, 2 * i + h + 1)
                    for b in range(HALF):
                        last = nc.tensor.transpose(ps_t[h][:, b, :], xn[:, h * HALF + b, :], ident[:])
                    last.then_inc(xnT_ps, 1)
                for h in range(2):
                    pe.wait_ge(xnT_ok, 2 * i + h + 1)
                    if not fresh:
                        pe.wait_ge(u_read, 2 * i + h - 1)
                    nc.tensor.matmul(ps_u[h][:], a2rep[:], xnT[:, half(h), :], start=True, stop=False)
                    for b in range(HALF):
                        last = nc.tensor.matmul(ps_u[h][:, b, :], xnT[:, h * HALF + b, :], a1rep[:],
                                                start=False, stop=(b == HALF - 1))
                    last.then_inc(u_ps, 1)
                    if not fresh or h:
                        pe.wait_ge(wh_ok, 2 * i + h)
                    for b in range(HALF):
                        last = nc.tensor.matmul(ps_wh[:, b, :], xnT[:, h * HALF + b, :], gw[:], start=True, stop=True)
                    last.then_inc(wh_ps, 1)

            def pe_ranks(pe, i):
                pe.wait_ge(both_ok, i + 1)
                rank = ps_m[:, 1, :]
                nc.tensor.matmul(rank, tri[:], both[:], start=True, stop=False)
                for s in range(1, OCT):
                    nc.tensor.matmul(rank[:, s * E:], ones[:], both[:, 0:OCT - s, :], start=False, stop=False)
                nc.tensor.matmul(rank.rearrange("p (b e) -> p b e", e=E), ones[:],
                                 taken[:].unsqueeze(1).to_broadcast([P, OCT, E]),
                                 start=False, stop=True).then_inc(rank_ps, 1)

            def pe_body(pe, i, r, first, last_one):
                for h in range(2):
                    pe.wait_ge(ex_ok, 2 * i + h + 1)
                    for b in range(HALF):
                        last = nc.tensor.transpose(ps_t[h][:, b, :], ex[:, h * HALF + b, :], ident[:])
                    last.then_inc(prT_ps, 1)
                for h in range(2):
                    pe.wait_ge(prT_ok, 2 * i + h + 1)
                    pe.wait_ge(wh_ok, 2 * i + h + 1)
                    if not first:
                        pe.wait_ge(h_read, 2 * i + h - 1)
                    for b in range(HALF):
                        k = h * HALF + b
                        last = nc.tensor.matmul(ps_h[h][:, b, :], prT[:, k, :], wh[:, k, :], start=True, stop=True)
                    last.then_inc(h_ps, 1)
                if not first:
                    pe_ranks(pe, i - 1)
                if not last_one:
                    pe_front(pe, i + 1, False)
                for h in range(2):
                    pe.wait_ge(xh_ok, 2 * i + h + 1)
                    for b in range(HALF):
                        last = nc.tensor.transpose(ps_t[h][:, b, :], stage[r][:, 0, h * HALF + b, 0:D], ident[:])
                    last.then_inc(xhT_ps, 1)
                for h in range(2):
                    pe.wait_ge(xhT_ok, 2 * i + h + 1)
                    if not first and h == 0:
                        pe.wait_ge(lg_read, i)
                    for b in range(HALF):
                        k = h * HALF + b
                        last = nc.tensor.matmul(ps_m[:, 0, k * E:(k + 1) * E], xhT[:, k, :], wrs[:],
                                                start=True, stop=True)
                last.then_inc(lg_ps, 1)

            def act_front(act, i, fresh):
                act.wait_ge(var1_ok, i + 1)
                nc.scalar.activation(seed1[:], var1[:], ACT.Ln).then_inc(ln1_ok, 1)
                act.wait_ge(ln1_ok, i + 1)
                nc.scalar.activation(seed1[:], seed1[:], ACT.Exp, scale=-0.5).then_inc(seed1_ok, 1)
                for h in range(2):
                    act.wait_ge(xnT_ps, 2 * i + h + 1)
                    if not fresh:
                        act.wait_ge(wh_ps, 2 * i + h - 1)
                    nc.scalar.copy(xnT[:, half(h), :], ps_t[h][:]).then_inc(xnT_ok, 1)
                for h in range(2):
                    act.wait_ge(wh_ps, 2 * i + h + 1)
                    if not fresh:
                        act.wait_ge(h_ps, 2 * i + h - 1)
                    nc.scalar.copy(wh[:, half(h), :], ps_wh[:]).then_inc(wh_ok, 1)

            def act_back(act, i):
                act.wait_ge(gap_ok, i + 1)
                nc.scalar.activation(egap[:], gap[:], ACT.Exp).then_inc(egap_ok, 1)

            def act_body(act, i, r, first, last_one):
                for h in range(2):
                    act.wait_ge(e_ok, 2 * i + h + 1)
                    for b in range(HALF):
                        k = h * HALF + b
                        last = nc.scalar.activation(ex[:, k, :], ex[:, k, :], ACT.Exp, bias=nbig[:, k:k + 1],
                                                    accum_out=den[:, k:k + 1])
                    last.then_inc(ex_ok, 1)
                for h in range(2):
                    act.wait_ge(prT_ps, 2 * i + h + 1)
                    if not first:
                        act.wait_ge(h_ps, 2 * i + h - 1)
                    nc.scalar.copy(prT[:, half(h), :], ps_t[h][:]).then_inc(prT_ok, 1)
                if not first:
                    act_back(act, i - 1)
                if not last_one:
                    act_front(act, i + 1, False)
                act.wait_ge(var2_ok, i + 1)
                nc.scalar.activation(seed2[:], var2[:], ACT.Ln).then_inc(ln2_ok, 1)
                act.wait_ge(ln2_ok, i + 1)
                nc.scalar.activation(seed2[:], seed2[:], ACT.Exp, scale=-0.5).then_inc(seed2_ok, 1)
                for h in range(2):
                    act.wait_ge(xhT_ps, 2 * i + h + 1)
                    if not first and h == 0:
                        act.wait_ge(lg_ps, i)
                    nc.scalar.copy(xhT[:, half(h), :], ps_t[h][:]).then_inc(xhT_ok, 1)
                act.wait_ge(xh_ok, 2 * i + 2)
                nc.scalar.copy(stage[r][:, 1, :, 0:D], stage[r][:, 0, :, 0:D]).then_inc(copied, 1)

            def pool_back(pool, i, r):
                wait_apart(pool, slots_ok, i + 1, passed_pool)
                wait_apart(pool, copied, i + 1, passed_pool)
                for k in range(2):
                    for b in range(OCT):
                        nc.gpsimd.indirect_dma_start(
                            out=rows_dram, out_offset=bass.IndirectOffsetOnAxis(ap=slots[r][:, k, b:b + 1], axis=0),
                            in_=stage[r][:, k, b, :], in_offset=None).then_inc(scattered[r], 16)

            class Chain:

                def __init__(self, dve):
                    self.dve, self.n = dve, 0
                    dve.sem_clear(step)

                def link(self, ins):
                    self.n += 1
                    ins.then_inc(step, 1)
                    self.dve.wait_ge(step, self.n)

            def newton(chain, root, seed, var, scratch):
                chain.link(nc.vector.tensor_tensor(scratch, seed, seed, ALU.mult))
                chain.link(nc.vector.scalar_tensor_tensor(scratch, scratch, -0.5, var, ALU.mult, ALU.mult))
                chain.link(nc.vector.scalar_tensor_tensor(root, scratch, 1.5, seed, ALU.add, ALU.mult))

            def dve_stats1(dve, chain, i):
                for b in range(OCT):
                    last = nc.vector.bn_stats(bn[:, b, :], tok[:, ds(i * OCT + b, 1), :])
                chain.link(last)
                for b in range(OCT):
                    last = nc.vector.bn_aggr(mv[:, b, :], bn[:, b, :])
                chain.link(last)
                nc.vector.tensor_scalar(var1[:], mv[:, :, 1], EPS, None, ALU.add).then_inc(var1_ok, 1)

            def dve_norm1(dve, chain, i, fresh):
                dve.wait_ge(seed1_ok, i + 1)
                newton(chain, root1[:], seed1[:], var1[:], tiny[:, 0, :])
                for h in range(2):
                    if not fresh:
                        dve.wait_ge(xnT_ps, 2 * i + h - 1)
                    for b in range(h * HALF, (h + 1) * HALF):
                        last = nc.vector.tensor_scalar(xn[:, b, :], tok[:, ds(i * OCT + b, 1), :].squeeze(1),
                                                       mv[:, b, 0:1], root1[:, b:b + 1], ALU.subtract, ALU.mult)
                    last.then_inc(xn_ok, 1)

            def dve_scores(dve, chain, i, first):
                for h in range(2):
                    wait_apart(dve, u_ps, 2 * i + h + 1, passed_dve)
                    for b in range(HALF):
                        k = h * HALF + b
                        last = nc.vector.tensor_tensor_reduce(out=um[:, k, :], in0=ps_u[h][:, b, :], in1=mask[:],
                                                              scale=1.0, scalar=LOWEST, op0=ALU.add, op1=ALU.max,
                                                              accum_out=top[:, k:k + 1])
                    last.then_inc(u_read, 1)
                dve.wait_ge(u_read, 2 * i + 2)
                chain.link(nc.vector.tensor_scalar(ntop[:], top[:], -1.0, None, ALU.mult))
                chain.link(nc.vector.scalar_tensor_tensor(nbig[:], ntop[:], SLOPE, ntop[:], ALU.mult, ALU.min))
                for h in range(2):
                    if not first:
                        dve.wait_ge(prT_ps, 2 * i + h - 1)
                    nc.vector.scalar_tensor_tensor(ex[:, half(h), :], um[:, half(h), :], SLOPE, um[:, half(h), :],
                                                   ALU.mult, ALU.max).then_inc(e_ok, 1)

            def dve_residual(dve, chain, i):
                dve.wait_ge(ex_ok, 2 * i + 2)
                chain.link(nc.vector.reciprocal(rden[:], den[:]))
                for h in range(2):
                    dve.wait_ge(h_ps, 2 * i + h + 1)
                    for b in range(HALF):
                        k = h * HALF + b
                        t = tok[:, ds(i * OCT + k, 1), :].squeeze(1)
                        last = nc.vector.scalar_tensor_tensor(t, ps_h[h][:, b, :], rden[:, k:k + 1], t,
                                                              ALU.mult, ALU.add)
                    last.then_inc(h_read, 1)

            def dve_stats2(dve, chain, i):
                wait_apart(dve, h_read, 2 * i + 2, passed_dve)
                for b in range(OCT):
                    last = nc.vector.bn_stats(bn2[:, b, :], tok[:, ds(i * OCT + b, 1), :])
                chain.link(last)
                for b in range(OCT):
                    last = nc.vector.bn_aggr(mv2[:, b, :], bn2[:, b, :])
                chain.link(last)
                chain.link(nc.vector.tensor_scalar(var2[:, 0, :], mv2[:, :, 1], EPS, None, ALU.add))
                nc.vector.scalar_tensor_tensor(var2[:, 1, :], var2[:, 0, :], EPS, mv2[:, :, 1],
                                               ALU.mult, ALU.add).then_inc(var2_ok, 1)

            def dve_norm2(dve, chain, i, r, turn):
                dve.wait_ge(seed2_ok, i + 1)
                newton(chain, root2[:], seed2[:], var2[:], tiny[:])
                chain.link(nc.vector.tensor_tensor(ratio[:], var2[:, 1, :], root2[:, 1, :], ALU.mult))
                chain.link(nc.vector.tensor_tensor(ratio[:], ratio[:], root2[:, 0, :], ALU.mult))
                if turn is not None:
                    dve.wait_ge(scattered[r], 16 * 2 * OCT * turn)
                for h in range(2):
                    for b in range(h * HALF, (h + 1) * HALF):
                        last = nc.vector.tensor_scalar(stage[r][:, 0, b, 0:D], tok[:, ds(i * OCT + b, 1), :].squeeze(1),
                                                       mv2[:, b, 0:1], root2[:, 1, b:b + 1], ALU.subtract, ALU.mult)
                    last.then_inc(xh_ok, 1)

            def dve_choose(dve, chain, i):
                def wide(v):
                    return v.unsqueeze(2).to_broadcast([P, OCT, E])

                def each(v):
                    return v.unsqueeze(1).to_broadcast([P, OCT, E])

                dve.wait_ge(lg_ps, i + 1)
                ins = nc.vector.tensor_tensor(lg[:], ps_m[:, 0, :].rearrange("p (b e) -> p b e", e=E), wide(ratio[:]),
                                              ALU.mult)
                ins.then_inc(lg_read, 1)
                dve.wait_ge(lg_read, i + 1)
                chain.link(nc.vector.tensor_tensor(lg[:], lg[:], each(brs[:]), ALU.add))
                for k, src in enumerate((lg, lg2)):
                    chain.link(nc.vector.tensor_reduce(best[:, k, :], src[:], AX.X, ALU.max))
                    chain.link(nc.vector.tensor_tensor(eq[:], src[:], wide(best[:, k, :]), ALU.is_equal))
                    chain.link(nc.vector.tensor_tensor(eq[:], eq[:], each(ranked[:]), ALU.mult))
                    chain.link(nc.vector.tensor_reduce(pick[:], eq[:], AX.X, ALU.max))
                    chain.link(nc.vector.tensor_tensor(hot[:, k], wide(pick[:]), each(ranked[:]), ALU.is_equal))
                    if k == 0:
                        chain.link(nc.vector.scalar_tensor_tensor(lg2[:], hot[:, 0], LOWEST, lg[:],
                                                                  ALU.mult, ALU.add))
                nc.vector.tensor_tensor(both[:], hot[:, 0], hot[:, 1], ALU.add).then_inc(both_ok, 1)
                nc.vector.tensor_tensor(gap[:], best[:, 1, :], best[:, 0, :], ALU.subtract).then_inc(gap_ok, 1)

            def dve_place(dve, chain, i, r):
                dve.wait_ge(rank_ps, i + 1)
                chain.link(nc.vector.tensor_tensor(place[:], ps_m[:, 1, :].rearrange("p (b e) -> p b e", e=E),
                                                   region[:].unsqueeze(1).to_broadcast([P, OCT, E]), ALU.add))
                chain.link(nc.vector.tensor_tensor(
                    chosen[:].rearrange("p k b e -> p k (b e)"), hot[:].rearrange("p k b e -> p k (b e)"),
                    place[:].rearrange("p b e -> p (b e)").unsqueeze(1).to_broadcast([P, 2, OCT * E]), ALU.mult))
                with nc.allow_low_precision(reason="one term of each sum is not zero, a whole number below 2^24"):
                    nc.vector.tensor_reduce(slots[r][:], chosen[:], AX.X, ALU.add)
                nc.vector.tensor_copy(stage[r][:, :, :, D].bitcast(I32), ids[:, :, ds(i * OCT, OCT)])
                dve.wait_ge(egap_ok, i + 1)
                chain.link(nc.vector.tensor_scalar(share[:], egap[:], 1.0, None, ALU.add))
                chain.link(nc.vector.reciprocal(stage[r][:, 0, :, D + 1], share[:]))
                nc.vector.tensor_tensor(stage[r][:, 1, :, D + 1], egap[:], stage[r][:, 0, :, D + 1],
                                        ALU.mult).then_inc(slots_ok, 1)
                chain.link(nc.vector.tensor_reduce(new[:], both[:].rearrange("p b e -> p e b"), AX.X, ALU.add))
                chain.link(nc.vector.tensor_tensor(taken[:], taken[:], new[:], ALU.add))

            def dve_body(dve, i, r, turn, first, last_one):
                chain = Chain(dve)
                dve_scores(dve, chain, i, first)
                if not first:
                    dve_choose(dve, chain, i - 1)
                if not last_one:
                    dve_stats1(dve, chain, i + 1)
                dve_residual(dve, chain, i)
                if not last_one:
                    dve_norm1(dve, chain, i + 1, False)
                dve_stats2(dve, chain, i)
                if not first:
                    dve_place(dve, chain, i - 1, 1 - r)
                dve_norm2(dve, chain, i, r, turn)

            PAIRS = (NO - 4) // 2

            with nc.Block() as block:
                @block.tensor
                def _(pe):
                    pe_front(pe, 0, True)
                    pe_body(pe, 0, 0, True, False)
                    pe_body(pe, 1, 1, False, False)
                    with pe.Fori(0, PAIRS) as n:
                        for r in range(2):
                            pe_body(pe, 2 * n + 2 + r, r, False, False)
                    pe_body(pe, NO - 2, 0, False, False)
                    pe_body(pe, NO - 1, 1, False, True)
                    pe_ranks(pe, NO - 1)

                @block.scalar
                def _(act):
                    act_front(act, 0, True)
                    act_body(act, 0, 0, True, False)
                    act_body(act, 1, 1, False, False)
                    with act.Fori(0, PAIRS) as n:
                        for r in range(2):
                            act_body(act, 2 * n + 2 + r, r, False, False)
                    act_body(act, NO - 2, 0, False, False)
                    act_body(act, NO - 1, 1, False, True)
                    act_back(act, NO - 1)

                @block.gpsimd
                def _(pool):
                    pool_back(pool, 0, 0)
                    with pool.Fori(0, PAIRS) as n:
                        for r in range(2):
                            pool_back(pool, 2 * n + 1 + r, 1 - r)
                    for i in range(2 * PAIRS + 1, NO):
                        pool_back(pool, i, i % 2)
                    for r in range(2):
                        pool.wait_ge(scattered[r], 16 * 2 * OCT * (NO // 2))

                @block.vector
                def _(dve):
                    chain = Chain(dve)
                    dve_stats1(dve, chain, 0)
                    dve_norm1(dve, chain, 0, True)
                    dve_body(dve, 0, 0, None, True, False)
                    dve_body(dve, 1, 1, None, False, False)
                    with dve.Fori(0, PAIRS) as n:
                        for r in range(2):
                            dve_body(dve, 2 * n + 2 + r, r, n + 1, False, False)
                    dve_body(dve, NO - 2, 0, NO // 2 - 1, False, False)
                    dve_body(dve, NO - 1, 1, NO // 2 - 1, False, True)
                    chain = Chain(dve)
                    dve_choose(dve, chain, NO - 1)
                    dve_place(dve, chain, NO - 1, 1)

        with ExitStack() as ctx:
            def sb(name, shape, dt=F32):
                return ctx.enter_context(nc.sbuf_tensor(name, shape, dt))

            def sem(name):
                return ctx.enter_context(nc.semaphore(name))

            KT = TOKENS // TILE
            count = sb("count", [1, E])
            fills = sb("fills_", [1, E, KT])
            kth = sb("kth", [1, KT])
            tiles = sb("tiles", [1, E])
            ends = sb("ends", [1, E])
            jth = sb("jth", [1, NT])
            past = sb("past", [1, NT, E])
            skip = sb("skip", [1, NT, E])
            who = sb("who", [1, NT])
            before = sb("before", [1, NT])
            rowf = sb("rowf", [1, NT])
            ps_n = ctx.enter_context(nc.psum_tensor("ps_n", [P, E], F32))

            count_ps = sem("count_ps")
            iotas = sem("iotas2")
            tails_ok = sem("tails_ok")
            table_ok = sem("table_ok")
            padded = sem("padded")
            step = sem("step2")

            with nc.Block() as block:
                @block.gpsimd
                def _(pool):
                    nc.gpsimd.iota(kth[:], pattern=[[TILE, KT]], base=0, channel_multiplier=0,
                                   allow_small_or_imprecise_dtypes=True).then_inc(iotas, 1)
                    nc.gpsimd.iota(jth[:], pattern=[[1, NT]], base=0, channel_multiplier=0,
                                   allow_small_or_imprecise_dtypes=True).then_inc(iotas, 1)

                @block.tensor
                def _(pe):
                    nc.tensor.matmul(ps_n[:], ones[:], taken[:], start=True, stop=True).then_inc(count_ps, 1)

                @block.sync
                def _(sp):
                    sp.wait_ge(tails_ok, 1)
                    for e in range(E):
                        row = sp.value_load(tails[0:1, e:e + 1], min_val=e * CAP, max_val=e * CAP + TOKENS)
                        sp.dma_start(rows_dram[bass.ds(row, TILE), :],
                                     pads_dram[e * TILE:(e + 1) * TILE, :]).then_inc(padded, 16)
                    sp.wait_ge(padded, 16 * E)

                @block.vector
                def _(dve):
                    steps = [0]

                    def link(ins):
                        steps[0] += 1
                        ins.then_inc(step, 1)
                        dve.wait_ge(step, steps[0])

                    dve.wait_ge(count_ps, 1)
                    link(nc.vector.tensor_copy(count[:], ps_n[0:1, :]))
                    nc.vector.tensor_tensor(tails[:], count[:], region[0:1, :], ALU.add).then_inc(tails_ok, 1)
                    dve.wait_ge(iotas, 2)
                    link(nc.vector.tensor_tensor(fills[:], count[:].unsqueeze(2).to_broadcast([1, E, KT]),
                                                 kth[:].unsqueeze(1).to_broadcast([1, E, KT]), ALU.is_gt))
                    link(nc.vector.tensor_reduce(tiles[:], fills[:], AX.X, ALU.add))
                    link(nc.vector.tensor_copy(ends[:, 0:1], tiles[:, 0:1]))
                    for e in range(1, E):
                        link(nc.vector.tensor_tensor(ends[:, e:e + 1], ends[:, e - 1:e], tiles[:, e:e + 1], ALU.add))
                    link(nc.vector.tensor_tensor(past[:], jth[:].unsqueeze(2).to_broadcast([1, NT, E]),
                                                 ends[:].unsqueeze(1).to_broadcast([1, NT, E]), ALU.is_ge))
                    link(nc.vector.tensor_reduce(who[:], past[:], AX.X, ALU.add))
                    link(nc.vector.tensor_tensor(skip[:], past[:], tiles[:].unsqueeze(1).to_broadcast([1, NT, E]),
                                                 ALU.mult))
                    link(nc.vector.tensor_reduce(before[:], skip[:], AX.X, ALU.add))
                    link(nc.vector.tensor_tensor(rowf[:], jth[:], before[:], ALU.subtract))
                    link(nc.vector.tensor_scalar(rowf[:], rowf[:], float(TILE), None, ALU.mult))
                    link(nc.vector.scalar_tensor_tensor(table[:, 0, :], who[:], float(CAP), rowf[:],
                                                        ALU.mult, ALU.add))
                    link(nc.vector.tensor_scalar(who[:], who[:], float(E - 1), None, ALU.min))
                    link(nc.vector.tensor_copy(table[:, 1, :], who[:]))
                    nc.vector.tensor_scalar(table[:, 2, :], who[:], float(HC + 1), None,
                                            ALU.mult).then_inc(table_ok, 1)
                    dve.wait_ge(table_ok, 1)

        before_experts.close()

        with ExitStack() as ctx:
            def sb(name, shape, dt=F32):
                return ctx.enter_context(nc.sbuf_tensor(name, shape, dt))

            def ps(name, shape):
                return ctx.enter_context(nc.psum_tensor(name, shape, F32))

            def sem(name):
                return ctx.enter_context(nc.semaphore(name))

            XB = 2
            xs = [sb(f"xs{n}", [P, CH, R]) for n in range(XB)]
            w1c = [sb(f"w1c{r}", [P, 2, H], F32R) for r in range(2)]
            w2c = [sb(f"w2c{r}", [P, 2, HC * D], F32R) for r in range(2)]
            xT = [sb(f"xT{r}", [P, 2, TILE], F32R) for r in range(2)]
            hf = [sb(f"hf{c}", [P, TILE]) for c in range(HC)]
            hs = [sb(f"hs{r}", [P, 2, HC, TILE], F32R) for r in range(2)]
            yT = sb("yT", [P, TILE])
            ys = [sb(f"ys{r}", [P, CH, D]) for r in range(2)]
            yid = [sb(f"yid{r}", [P, CH], I32) for r in range(2)]
            tile_id = [sb(f"tile_id{n}", [P, CH], I32) for n in range(4)]
            tile_wt = [sb(f"tile_wt{n}", [P, CH]) for n in range(4)]
            ps_x = ps("ps_x", [P, CH, P])
            ps_l1 = [ps(f"ps_l1_{c}", [P, TILE]) for c in range(HC)]
            ps_l2 = ps("ps_l2", [P, TILE])
            ps_y = ps("ps_y", [P, CH, D])

            x_in = [sem(f"x_in{r}") for r in range(XB)]
            w1_in = [sem(f"w1_in{r}") for r in range(2)]
            w2_in = [sem(f"w2_in{r}") for r in range(2)]
            x_ps = sem("x_ps")
            xhigh_ok = sem("xhigh_ok")
            xlow_ok = sem("xlow_ok")
            l1_ps = sem("l1_ps")
            gelu_ok = sem("gelu_ok")
            high_ok = sem("high_ok")
            acthigh_ok = sem("acthigh_ok")
            low_ok = sem("low_ok")
            l2_ps = sem("l2_ps")
            yT_ok = sem("yT_ok")
            y_ps = sem("y_ps")
            ys_ok = sem("ys_ok")
            tails_ok = sem("tails_kept")
            yid_ok = sem("yid_ok")
            passed = sem("passed")
            sent = [sem(f"sent{r}") for r in range(2)]


            def pe_x(pe, t, q, turn):
                pe.wait_ge(x_in[q % 2], 32 * turn + 16 * (q // 2) + 16)
                if not isinstance(t, int) or t >= 1:
                    pe.wait_ge(xlow_ok, t)
                for c in range(CH):
                    last = nc.tensor.transpose(ps_x[:, c, :], xs[q % 2][:, c, 0:D], ident[:])
                last.then_inc(x_ps, 1)

            def pe_layer1(pe, t, q, turn, c):
                r = q % 2
                if c == 0:
                    pe.wait_ge(w1_in[r], 32 * turn + 16 * (q // 2) + 16)
                    pe.wait_ge(xlow_ok, t + 1)
                if not isinstance(t, int) or t >= 1:
                    pe.wait_ge(gelu_ok, HC * t + c - HC + 1)
                for n, (a, b) in enumerate(((0, 0), (0, 1), (1, 0))):
                    last = nc.tensor.matmul(ps_l1[c][:], w1c[r][:, a, c * P:(c + 1) * P], xT[r][:, b, :],
                                            start=(n == 0), stop=(n == 2))
                last.then_inc(l1_ps, 1)

            def pe_layer2(pe, t, q, turn):
                r = q % 2
                pe.wait_ge(w2_in[r], 32 * turn + 16 * (q // 2) + 16)
                if not isinstance(t, int) or t >= 1:
                    pe.wait_ge(yT_ok, t)
                for c in range(HC):
                    pe.wait_ge(low_ok, HC * t + c + 1)
                    for n, (a, b) in enumerate(((0, 0), (0, 1), (1, 0))):
                        last = nc.tensor.matmul(ps_l2[:], w2c[r][:, a, c * D:(c + 1) * D], hs[r][:, b, c, :],
                                                start=(c == 0 and n == 0), stop=(c == HC - 1 and n == 2))
                last.then_inc(l2_ps, 1)

            def pe_y(pe, t):
                pe.wait_ge(yT_ok, t + 1)
                if not isinstance(t, int) or t >= 1:
                    pe.wait_ge(ys_ok, t)
                for c in range(CH):
                    last = nc.tensor.transpose(ps_y[:, c, :], yT[:, c * P:(c + 1) * P], ident[:])
                last.then_inc(y_ps, 1)

            def act_x(act, t, q):
                act.wait_ge(x_ps, t + 1)
                if not isinstance(t, int) or t >= 2:
                    act.wait_ge(l1_ps, HC * t - HC)
                nc.scalar.copy(xT[q % 2][:, 0, :], ps_x[:].rearrange("p c n -> p (c n)")).then_inc(xhigh_ok, 1)

            def act_gelu(act, t, c, column):
                act.wait_ge(l1_ps, HC * t + c + 1)
                if not isinstance(t, int) or t >= 1:
                    act.wait_ge(low_ok, HC * t + c - HC + 1)
                nc.scalar.activation(hf[c][:], ps_l1[c][:], ACT.Gelu,
                                     bias=biases[:, ds(column + c, 1)]).then_inc(gelu_ok, 1)

            def act_high(act, t, q, c):
                act.wait_ge(gelu_ok, HC * t + c + 1)
                if not isinstance(t, int) or t >= 2:
                    act.wait_ge(l2_ps, t - 1)
                nc.scalar.copy(hs[q % 2][:, 0, c, :], hf[c][:]).then_inc(acthigh_ok, 1)

            def act_y(act, t, column):
                act.wait_ge(l2_ps, t + 1)
                if not isinstance(t, int) or t >= 1:
                    act.wait_ge(y_ps, t)
                nc.scalar.activation(yT[:], ps_l2[:], ACT.Identity,
                                     bias=biases[:, ds(column + HC, 1)]).then_inc(yT_ok, 1)

            def dve_x(dve, t, q, turn):
                dve.wait_ge(x_in[q % 2], 32 * turn + 16 * (q // 2) + 16)
                if not isinstance(t, int) or t >= 4:
                    dve.wait_ge(ys_ok, t - 3)
                nc.vector.tensor_copy(tile_id[q][:], xs[q % 2][:, :, D].bitcast(I32)).then_inc(tails_ok, 1)
                nc.vector.tensor_copy(tile_wt[q][:], xs[q % 2][:, :, D + 1]).then_inc(tails_ok, 1)
                dve.wait_ge(xhigh_ok, t + 1)
                if not isinstance(t, int) or t >= 2:
                    dve.wait_ge(l1_ps, HC * t - HC)
                nc.vector.tensor_tensor(xT[q % 2][:, 1, :], ps_x[:].rearrange("p c n -> p (c n)"),
                                        xT[q % 2][:, 0, :].bitcast(F32), ALU.subtract).then_inc(xlow_ok, 1)

            def dve_high(dve, t, q, c):
                dve.wait_ge(gelu_ok, HC * t + c + 1)
                if not isinstance(t, int) or t >= 2:
                    dve.wait_ge(l2_ps, t - 1)
                nc.vector.tensor_copy(hs[q % 2][:, 0, c, :], hf[c][:]).then_inc(high_ok, 1)

            def dve_low(dve, t, q, c):
                if c % 2:
                    dve.wait_ge(acthigh_ok, HC // 2 * t + c // 2 + 1)
                else:
                    dve.wait_ge(high_ok, HC // 2 * t + c // 2 + 1)
                nc.vector.tensor_tensor(hs[q % 2][:, 1, c, :], hf[c][:], hs[q % 2][:, 0, c, :].bitcast(F32),
                                        ALU.subtract).then_inc(low_ok, 1)

            def dve_y(dve, t, q, turn):
                r = q % 2
                dve.wait_ge(y_ps, t + 1)
                if not isinstance(t, int) or t >= 2:
                    dve.wait_ge(sent[r], 16 * CH * 2 * turn + 16 * CH * (q // 2))
                dve.wait_ge(tails_ok, 2 * t + 2)
                nc.vector.tensor_copy(yid[r][:], tile_id[q][:]).then_inc(yid_ok, 1)
                nc.vector.tensor_tensor(ys[r][:], ps_y[:], tile_wt[q][:].unsqueeze(2).to_broadcast([P, CH, D]),
                                        ALU.mult).then_inc(ys_ok, 1)

            def pool_y(pool, t, q):
                wait_apart(pool, ys_ok, t + 1, passed)
                wait_apart(pool, yid_ok, t + 1, passed)
                for c in range(CH):
                    nc.gpsimd.indirect_dma_start(
                        out=y_dram, out_offset=bass.IndirectOffsetOnAxis(ap=yid[q % 2][:, c:c + 1], axis=0),
                        in_=ys[q % 2][:, c, :], in_offset=None).then_inc(sent[q % 2], 16)

            def sp_x(sp, t, q):
                row = sp.value_load(table[0:1, 0, ds(t, 1)], min_val=0, max_val=E * CAP + (DEAD - 1) * TILE)
                if not isinstance(t, int) or t >= XB:
                    sp.wait_ge(x_ps, t - XB + 1)
                    sp.wait_ge(tails_ok, 2 * (t - XB) + 2)
                sp.dma_start(xs[q % 2][:], rows_dram[bass.ds(row, TILE), :].rearrange("(c p) r -> p c r", p=P)
                             ).then_inc(x_in[q % 2], 16)

            def sp_w1(sp, t, q):
                e = sp.value_load(table[0:1, 1, ds(t, 1)], min_val=0, max_val=E - 1)
                if not isinstance(t, int) or t >= 2:
                    sp.wait_ge(l1_ps, HC * t - HC)
                sp.dma_start(w1c[q % 2][:].rearrange("p a h -> p (a h)").bitcast(F32),
                             w1all[:, bass.ds(e * (2 * H), 2 * H)]).then_inc(w1_in[q % 2], 16)

            def sp_w2(sp, t, q):
                e = sp.value_load(table[0:1, 1, ds(t, 1)], min_val=0, max_val=E - 1)
                if not isinstance(t, int) or t >= 2:
                    sp.wait_ge(l2_ps, t - 1)
                sp.dma_start(w2c[q % 2][:].rearrange("p a h -> p (a h)").bitcast(F32),
                             w2all[:, bass.ds(e * (2 * HC * D), 2 * HC * D)]).then_inc(w2_in[q % 2], 16)

            biases = bias[:].rearrange("p e c -> p (e c)")
            w1all = w1s[:].rearrange("p e a h -> p (e a h)").bitcast(F32)
            w2all = w2s[:].rearrange("p e a h -> p (e a h)").bitcast(F32)

            HEAD = 3
            LOOPS = (NT - HEAD - 1) // 4
            REST = HEAD + 4 * LOOPS

            def previous(q, turn, n):
                return (q - n) % 4, turn + (q - n) // 4

            def iterations(engine, step_of):
                for t in range(HEAD):
                    step_of(t, t % 4, t // 4)
                with engine.Fori(0, LOOPS) as n:
                    for k in range(4):
                        step_of(4 * n + (HEAD + k), (HEAD + k) % 4, n + (HEAD + k) // 4)
                for t in range(REST, NT + 2):
                    step_of(t, t % 4, t // 4)

            def present(t, low, high=NT):
                return not isinstance(t, int) or low <= t < high

            with nc.Block() as block:
                @block.gpsimd
                def _(pool):
                    def step_of(t, q, turn):
                        if present(t, 2, NT + 2):
                            pool_y(pool, t - 2, (q - 2) % 4)
                    iterations(pool, step_of)
                    for r in range(2):
                        pool.wait_ge(sent[r], 16 * CH * ((NT - r + 1) // 2))

                @block.sync
                def _(sp):
                    sp_x(sp, 0, 0)
                    sp_w1(sp, 0, 0)
                    sp_x(sp, 1, 1)
                    sp_w1(sp, 1, 1)
                    sp_w2(sp, 0, 0)

                    def step_of(t, q, turn):
                        if present(t, 0, NT - 2):
                            sp_x(sp, t + 2, (q + 2) % 4)
                            sp_w1(sp, t + 2, (q + 2) % 4)
                        if present(t, 0, NT - 1):
                            sp_w2(sp, t + 1, (q + 1) % 4)
                    iterations(sp, step_of)

                @block.tensor
                def _(pe):
                    pe_x(pe, 0, 0, 0)

                    def step_of(t, q, turn):
                        if present(t, 0):
                            pe_layer1(pe, t, q, turn, 0)
                            pe_layer1(pe, t, q, turn, 1)
                        if present(t, 0, NT - 1):
                            pe_x(pe, t + 1, (q + 1) % 4, turn + (q + 1) // 4)
                        if present(t, 0):
                            pe_layer1(pe, t, q, turn, 2)
                            pe_layer1(pe, t, q, turn, 3)
                        if present(t, 2, NT + 2):
                            pe_y(pe, t - 2)
                        if present(t, 1, NT + 1):
                            pe_layer2(pe, t - 1, *previous(q, turn, 1))
                    iterations(pe, step_of)

                @block.scalar
                def _(act):
                    act_x(act, 0, 0)

                    def step_of(t, q, turn):
                        if present(t, 2, NT + 2):
                            column = act.value_load(table[0:1, 2, ds(t - 2, 1)], min_val=0, max_val=(E - 1) * (HC + 1))
                            act_y(act, t - 2, column)
                        if present(t, 0):
                            column = act.value_load(table[0:1, 2, ds(t, 1)], min_val=0, max_val=(E - 1) * (HC + 1))
                            act_gelu(act, t, 0, column)
                            act_gelu(act, t, 1, column)
                            act_high(act, t, q, 1)
                        if present(t, 0, NT - 1):
                            act_x(act, t + 1, (q + 1) % 4)
                        if present(t, 0):
                            act_gelu(act, t, 2, column)
                            act_gelu(act, t, 3, column)
                            act_high(act, t, q, 3)
                    iterations(act, step_of)

                @block.vector
                def _(dve):
                    dve_x(dve, 0, 0, 0)

                    def step_of(t, q, turn):
                        if present(t, 0):
                            dve_high(dve, t, q, 0)
                            dve_low(dve, t, q, 0)
                            dve_low(dve, t, q, 1)
                        if present(t, 0, NT - 1):
                            dve_x(dve, t + 1, (q + 1) % 4, turn + (q + 1) // 4)
                        if present(t, 0):
                            dve_high(dve, t, q, 2)
                            dve_low(dve, t, q, 2)
                        if present(t, 2, NT + 2):
                            dve_y(dve, t - 2, *previous(q, turn, 2))
                        if present(t, 0):
                            dve_low(dve, t, q, 3)
                    iterations(dve, step_of)

        with ExitStack() as ctx:
            YB = 4
            yb = [ctx.enter_context(nc.sbuf_tensor(f"yb{n}", [P, OCT, 2, D], F32)) for n in range(YB)]
            y_in = [ctx.enter_context(nc.semaphore(f"y_in{n}")) for n in range(YB)]
            summed = ctx.enter_context(nc.semaphore("summed"))
            total = ctx.enter_context(nc.semaphore("total"))
            stored = ctx.enter_context(nc.semaphore("stored"))
            y_tokens = y_dram[0:ROWS, :].rearrange("(g p k) d -> p g k d", p=P, k=2)

            with nc.Block() as block:
                @block.sync
                def _(sp):
                    for o in range(NO):
                        if o >= YB:
                            sp.wait_ge(total, o - YB + 1)
                        sp.dma_start(yb[o % YB][:], y_tokens[:, o * OCT:(o + 1) * OCT]).then_inc(y_in[o % YB], 16)

                @block.vector
                def _(dve):
                    for o in range(NO):
                        g = slice(o * OCT, (o + 1) * OCT)
                        dve.wait_ge(y_in[o % YB], 16 * (o // YB + 1))
                        nc.vector.tensor_tensor(tok[:, g, :], tok[:, g, :], yb[o % YB][:, :, 0, :],
                                                ALU.add).then_inc(summed, 1)
                        dve.wait_ge(summed, o + 1)
                        nc.vector.tensor_tensor(tok[:, g, :], tok[:, g, :], yb[o % YB][:, :, 1, :],
                                                ALU.add).then_inc(total, 1)

                @block.scalar
                def _(act):
                    for o in range(NO):
                        g = slice(o * OCT, (o + 1) * OCT)
                        act.wait_ge(total, o + 1)
                        act.dma_start(out[g].rearrange("g p d -> p g d"), tok[:, g, :]).then_inc(stored, 16)
                    act.wait_ge(stored, 16 * NO)


_INS = ["x", "adj", "L0_gnn_W", "L0_gnn_a", "L0_ffn_Wr", "L0_ffn_br", "L0_ffn_ln_g", "L0_ffn_ln_b",
        "L0_ffn_W1", "L0_ffn_b1", "L0_ffn_W2", "L0_ffn_b2"]


def kernel(**inputs):
    import numpy as np
    import concourse.bacc as bacc
    from concourse.bass_utils import run_bass_kernel_spmd

    nc = bacc.Bacc("TRN2", target_bir_lowering=False, num_devices=1)
    arrays, args = {}, []
    for name in _INS:
        a = np.ascontiguousarray(inputs[name])
        arrays[f"in_{name}"] = a
        args.append(nc.dram_tensor(f"in_{name}", a.shape, mybir.dt.from_np(a.dtype), kind="ExternalInput").ap())
    shape = inputs["x"].shape
    out = nc.dram_tensor("out_0", shape, F32, kind="ExternalOutput").ap()
    moe_kernel(nc, *args, out)
    r = run_bass_kernel_spmd(nc, [arrays], core_ids=[0])
    return r.results[0]["out_0"]
```

```python
from contextlib import ExitStack

import concourse.bass as bass
from concourse import mybir

F32 = mybir.dt.float32
F32R = mybir.dt.float32r
BF16 = mybir.dt.bfloat16
I32 = mybir.dt.int32
ALU = mybir.AluOpType
ACT = mybir.ActivationFunctionType
AX = mybir.AxisListType

P = 128
OCT = 8
HALF = OCT // 2
TILE = 512
CH = TILE // P
EPS = 1e-5
SLOPE = 0.2
MASKED = -1e30
LOWEST = -3e38
ROOT_SEED = float(0x5f375980)


def moe_kernel(nc, x, adj, gnn_w, gnn_a, wr, br, ln_g, ln_b, w1, b1, w2, b2, out):
    G, N, D = x.shape
    E, _, H = w1.shape
    HC = H // P
    NO = G // OCT
    TOKENS = G * N
    ROWS = 2 * TOKENS
    NT = ROWS // TILE + E - 1
    DEAD = E - 1
    CAP = TOKENS + TILE
    R = D + 2
    assert N == P and D == P and G % OCT == 0 and H % P == 0 and ROWS % TILE == 0

    rows_dram = nc.dram_tensor("expert_rows", [E * CAP + DEAD * TILE, R], F32).ap()
    pads_dram = nc.dram_tensor("pad_rows", [E * TILE, R], F32).ap()
    y_dram = nc.dram_tensor("expert_out", [ROWS + (E + DEAD) * TILE, D], F32).ap()

    def wait_apart(engine, sem, value, passed):
        engine.wait_ge(sem, value)
        if not isinstance(value, int):
            engine.sem_inc(passed, 1)

    def ds(start, size):
        return slice(start, start + size) if isinstance(start, int) else bass.ds(start, size)

    with ExitStack() as whole:
        def keep(name, shape, dt=F32):
            return whole.enter_context(nc.sbuf_tensor(name, shape, dt))

        tok = keep("tok", [P, G, D])
        w1s = keep("w1s", [P, E, 2, H], F32R)
        w2s = keep("w2s", [P, E, 2, HC * D], F32R)
        bias = keep("bias", [P, E, HC + 1])
        ident = keep("ident", [P, P])
        table = keep("table", [1, 3, NT], I32)

        before_experts = whole.enter_context(ExitStack())

        def keep_to_plan(name, shape, dt=F32):
            return before_experts.enter_context(nc.sbuf_tensor(name, shape, dt))

        tri = keep_to_plan("tri", [P, P], BF16)
        ones = keep_to_plan("ones", [P, P], BF16)
        gw = keep_to_plan("gw", [P, D])
        a1rep = keep_to_plan("a1rep", [P, P])
        a2rep = keep_to_plan("a2rep", [P, P])
        mask = keep_to_plan("mask", [P, P])
        wrs = keep_to_plan("wrs", [P, E])
        brs = keep_to_plan("brs", [P, E])
        ranked = keep_to_plan("ranked", [P, E])
        region = keep_to_plan("region", [P, E])
        ids = keep_to_plan("ids", [P, 2, G], I32)
        taken = keep_to_plan("taken", [P, E], BF16)
        tails = keep_to_plan("tails", [1, E], I32)

        with ExitStack() as ctx:
            def sb(name, shape, dt=F32):
                return ctx.enter_context(nc.sbuf_tensor(name, shape, dt))

            def sem(name):
                return ctx.enter_context(nc.semaphore(name))

            w1raw = sb("w1raw", [P, E, H])
            w2raw = sb("w2raw", [P, E, HC * D])
            w1g = sb("w1g", [P, 2, H])
            adjs = sb("adjs", [P, P])
            arow = sb("arow", [P, 2, D])
            prod = sb("prod", [P, D])
            acol = sb("acol", [P, 2])
            NV = E * HC + 3 * E
            vecs = sb("vecs", [NV, P])
            cols = sb("cols", [P, NV])
            pads = sb("pads", [P, E + DEAD, CH, R])
            ps_cols = ctx.enter_context(nc.psum_tensor("ps_cols", [P, NV], F32))
            ps_b1 = ctx.enter_context(nc.psum_tensor("ps_b1", [P, E * HC], F32))
            B2, LG, LB = E * HC, E * HC + E, E * HC + 2 * E

            small_in = sem("small_in")
            tok_in = sem("tok_in")
            w1_in = sem("w1_in")
            w2_in = sem("w2_in")
            fills = sem("fills")
            ident_ok = sem("ident_ok")
            iotas = sem("iotas")
            pads_zero = sem("pads_zero")
            pads_ok = sem("pads_ok")
            pads_out = sem("pads_out")
            cols_ps = sem("cols_ps")
            cols_ok = sem("cols_ok")
            b1_ps = sem("b1_ps")
            bias_ok = sem("bias_ok")
            scaled = sem("scaled")
            high1 = sem("high1")
            low1 = sem("low1")
            high2 = sem("high2")
            low2 = sem("low2")
            acols = sem("acols")
            arep = sem("arep")
            step = sem("step")

            with nc.Block() as block:
                @block.sync
                def _(sp):
                    sp.dma_start(vecs[0:B2, :], b1.rearrange("e (c p) -> (e c) p", p=P)).then_inc(small_in, 16)
                    sp.dma_start(vecs[B2:LG, :], b2).then_inc(small_in, 16)
                    sp.dma_start(vecs[LG:LB, :], ln_g).then_inc(small_in, 16)
                    sp.dma_start(vecs[LB:NV, :], ln_b).then_inc(small_in, 16)
                    sp.dma_start(gw[:], gnn_w).then_inc(small_in, 16)
                    sp.dma_start(adjs[:], adj).then_inc(small_in, 16)
                    sp.dma_start(wrs[:], wr).then_inc(small_in, 16)
                    sp.dma_start(brs[:], br.partition_broadcast(P)).then_inc(small_in, 16)
                    for k in range(2):
                        a_k = gnn_a[k * D:(k + 1) * D, :].rearrange("d o -> (d o)")
                        sp.dma_start(arow[:, k, :], a_k.partition_broadcast(P)).then_inc(small_in, 16)
                    sp.dma_start(w1raw[:], w1.rearrange("e d h -> d e h")).then_inc(w1_in, 16)
                    sp.dma_start(w2raw[:].rearrange("p e (c d) -> p e c d", d=D),
                                 w2.rearrange("e (c p) d -> p e c d", p=P)).then_inc(w2_in, 16)
                    for n in range(4):
                        g0, g1 = n * G // 4, (n + 1) * G // 4
                        sp.dma_start(tok[:, g0:g1, :], x[g0:g1].rearrange("g p d -> p g d")).then_inc(tok_in, 16)
                    sp.wait_ge(pads_ok, 1)
                    sp.dma_start(pads_dram.rearrange("(e c p) r -> p e c r", p=P, c=CH),
                                 pads[:, 0:E]).then_inc(pads_out, 16)
                    sp.dma_start(rows_dram[E * CAP:, :].rearrange("(e c p) r -> p e c r", p=P, c=CH),
                                 pads[:, E:]).then_inc(pads_out, 16)
                    sp.wait_ge(pads_out, 32)
                    sp.wait_ge(tok_in, 64)

                @block.gpsimd
                def _(pool):
                    nc.gpsimd.memset(ident[:], 0.0).then_inc(fills, 1)
                    nc.gpsimd.memset(tri[:], 1.0).then_inc(fills, 1)
                    pool.wait_ge(fills, 2)
                    nc.gpsimd.affine_select(out=ident[:], in_=ident[:], compare_op=ALU.not_equal, fill=1.0, base=0,
                                            pattern=[[-1, P]], channel_multiplier=1).then_inc(ident_ok, 1)
                    nc.gpsimd.affine_select(out=tri[:], in_=tri[:], compare_op=ALU.is_gt, fill=0.0, base=0,
                                            pattern=[[1, P]], channel_multiplier=-1).then_inc(iotas, 1)
                    nc.gpsimd.iota(ids[:], pattern=[[1, 2], [2 * N, G]], base=0, channel_multiplier=2).then_inc(iotas, 1)
                    nc.gpsimd.iota(ranked[:], pattern=[[-1, E]], base=E, channel_multiplier=0,
                                   allow_small_or_imprecise_dtypes=True).then_inc(iotas, 1)
                    nc.gpsimd.iota(region[:], pattern=[[CAP, E]], base=0, channel_multiplier=0,
                                   allow_small_or_imprecise_dtypes=True).then_inc(iotas, 1)
                    nc.gpsimd.memset(pads[:], 0.0).then_inc(pads_zero, 1)
                    pool.wait_ge(pads_zero, 1)
                    nc.gpsimd.iota(pads[:, :, :, D:D + 1].bitcast(I32),
                                   pattern=[[TILE, E + DEAD], [P, CH], [1, 1]], base=ROWS,
                                   channel_multiplier=1).then_inc(pads_ok, 1)
                    pool.wait_ge(iotas, 4)

                @block.tensor
                def _(pe):
                    pe.wait_ge(small_in, 160)
                    pe.wait_ge(ident_ok, 1)
                    nc.tensor.transpose(ps_cols[:], vecs[:], ident[0:NV, 0:NV]).then_inc(cols_ps, 1)
                    pe.wait_ge(cols_ok, 1)
                    pe.wait_ge(w1_in, 16)
                    for e in range(E):
                        for c in range(HC):
                            mm = nc.tensor.matmul(ps_b1[:, e * HC + c:e * HC + c + 1], w1raw[:, e, c * P:(c + 1) * P],
                                                  cols[:, LB + e:LB + e + 1], start=True, stop=True)
                    mm.then_inc(b1_ps, 1)

                @block.scalar
                def _(act):
                    act.wait_ge(cols_ok, 1)
                    act.wait_ge(w1_in, 16)
                    for e in range(E):
                        if e >= 2:
                            act.wait_ge(low1, e - 1)
                        nc.scalar.activation(w1g[:, e % 2, :], w1raw[:, e, :], ACT.Copy,
                                             scale=cols[:, LG + e:LG + e + 1]).then_inc(scaled, 1)
                        act.wait_ge(scaled, e + 1)
                        nc.scalar.activation(w1s[:, e, 0, :], w1g[:, e % 2, :], ACT.Copy).then_inc(high1, 1)
                    act.wait_ge(w2_in, 16)
                    for e in range(E):
                        nc.scalar.activation(w2s[:, e, 0, :], w2raw[:, e, :], ACT.Copy).then_inc(high2, 1)

                @block.vector
                def _(dve):
                    steps = [0]

                    def link(ins):
                        steps[0] += 1
                        ins.then_inc(step, 1)
                        dve.wait_ge(step, steps[0])

                    nc.vector.memset(ones[:], 1.0)
                    nc.vector.memset(taken[:], 0.0)
                    dve.wait_ge(small_in, 160)
                    link(nc.vector.tensor_scalar(mask[:], adjs[:], 0.0, MASKED, ALU.is_equal, ALU.mult))
                    for k, rep in enumerate((a1rep, a2rep)):
                        link(nc.vector.tensor_tensor_reduce(out=prod[:], in0=gw[:], in1=arow[:, k, :], scale=1.0,
                                                            scalar=0.0, op0=ALU.mult, op1=ALU.add,
                                                            accum_out=acol[:, k:k + 1]))
                        link(nc.vector.tensor_copy(rep[:], acol[:, k:k + 1].to_broadcast([P, P])))
                    dve.wait_ge(cols_ps, 1)
                    nc.vector.tensor_copy(cols[:], ps_cols[:]).then_inc(cols_ok, 1)
                    dve.wait_ge(cols_ok, 1)
                    nc.vector.tensor_copy(bias[:, :, HC:HC + 1], cols[:, B2:LG].unsqueeze(2)).then_inc(bias_ok, 1)
                    dve.wait_ge(b1_ps, 1)
                    nc.vector.tensor_tensor(bias[:, :, 0:HC], ps_b1[:].rearrange("p (e c) -> p e c", c=HC),
                                            cols[:, 0:B2].rearrange("p (e c) -> p e c", c=HC),
                                            ALU.add).then_inc(bias_ok, 1)
                    for e in range(E):
                        dve.wait_ge(high1, e + 1)
                        nc.vector.tensor_tensor(w1s[:, e, 1, :], w1g[:, e % 2, :], w1s[:, e, 0, :].bitcast(F32),
                                                ALU.subtract).then_inc(low1, 1)
                    for e in range(E):
                        dve.wait_ge(high2, e + 1)
                        nc.vector.tensor_tensor(w2s[:, e, 1, :], w2raw[:, e, :], w2s[:, e, 0, :].bitcast(F32),
                                                ALU.subtract).then_inc(low2, 1)
                    dve.wait_ge(low2, E)
                    dve.wait_ge(bias_ok, 2)

        with ExitStack() as ctx:
            def sb(name, shape, dt=F32):
                return ctx.enter_context(nc.sbuf_tensor(name, shape, dt))

            def ps(name, shape):
                return ctx.enter_context(nc.psum_tensor(name, shape, F32))

            def sem(name):
                return ctx.enter_context(nc.semaphore(name))

            xn = sb("xn", [P, OCT, D])
            xnT = sb("xnT", [P, OCT, P])
            wh = [sb(f"wh{r}", [P, OCT, D]) for r in range(2)]
            um = sb("um", [P, OCT, P])
            ex = sb("ex", [P, OCT, P])
            prT = sb("prT", [P, OCT, P])
            xh = sb("xh", [P, OCT, D])
            xhT = sb("xhT", [P, OCT, P])
            stage = [sb(f"stage{r}", [P, 2, OCT, R]) for r in range(2)]
            slots = [sb(f"slots{r}", [P, 2, OCT], I32) for r in range(2)]
            bn = sb("bn", [P, OCT, 6])
            mv = [sb(f"mv{r}", [P, OCT, 2]) for r in range(2)]
            bn2 = sb("bn2", [P, OCT, 6])
            mv2 = sb("mv2", [P, OCT, 2])
            var = sb("var", [P, 3, OCT])
            tiny = sb("tiny", [P, 3, OCT])
            seed = sb("seed", [P, 3, OCT])
            root = sb("root", [P, 3, OCT])
            shift1 = sb("shift1", [P, OCT])
            root1 = sb("root1", [P, OCT])
            ratio = sb("ratio", [P, OCT])
            top = sb("top", [P, OCT])
            ntop = sb("ntop", [P, OCT])
            nbig = sb("nbig", [P, OCT])
            den = sb("den", [P, OCT])
            rden = sb("rden", [P, OCT])
            lg = sb("lg", [P, OCT, E])
            lg2 = sb("lg2", [P, OCT, E])
            eq = sb("eq", [P, OCT, E])
            hot = sb("hot", [P, 2, OCT, E])
            best = sb("best", [P, 2, OCT])
            pick = sb("pick", [P, OCT])
            both = sb("both", [P, OCT, E], BF16)
            place = sb("place", [P, OCT, E])
            chosen = sb("chosen", [P, 2, OCT, E])
            gap = sb("gap", [P, OCT])
            egap = sb("egap", [P, OCT])
            share = sb("share", [P, OCT])
            new = sb("new", [P, E])

            ps_t = [ps(f"ps_t{h}", [P, HALF, P]) for h in range(2)]
            ps_wh = ps("ps_wh", [P, HALF, D])
            ps_u = [ps(f"ps_u{h}", [P, HALF, P]) for h in range(2)]
            ps_h = [ps(f"ps_h{h}", [P, HALF, D]) for h in range(2)]
            ps_m = ps("ps_m", [P, 2, OCT * E])

            root1_ok = sem("root1_ok")
            xn_ok = sem("xn_ok")
            xnT_ps = sem("xnT_ps")
            xnT_ok = sem("xnT_ok")
            wh_ps = sem("wh_ps")
            wh_ok = sem("wh_ok")
            u_ps = sem("u_ps")
            u_read = sem("u_read")
            nbig_ok = sem("nbig_ok")
            e_ok = sem("e_ok")
            ex_ok = sem("ex_ok")
            prT_ps = sem("prT_ps")
            prT_ok = sem("prT_ok")
            h_ps = sem("h_ps")
            h_read = sem("h_read")
            xh_ok = sem("xh_ok")
            copied = sem("copied")
            passed_dve = sem("passed_dve")
            passed_pool = sem("passed_pool")
            xhT_ps = sem("xhT_ps")
            xhT_ok = sem("xhT_ok")
            lg_ps = sem("lg_ps")
            lg_read = sem("lg_read")
            gap_ok = sem("gap_ok")
            egap_ok = sem("egap_ok")
            both_ok = sem("both_ok")
            rank_ps = sem("rank_ps")
            rank_read = sem("rank_read")
            slots_ok = sem("slots_ok")
            scattered = [sem(f"scattered{r}") for r in range(2)]
            score_step = sem("score_step")
            moment1_step = sem("moment1_step")
            moment2_step = sem("moment2_step")
            root_step = sem("root_step")
            choice_step = sem("choice_step")
            place_step = sem("place_step")

            def half(h):
                return slice(h * HALF, (h + 1) * HALF)

            def graphs(h):
                return range(h * HALF, (h + 1) * HALF)

            def from_octet(j, first):
                return not isinstance(j, int) or j >= first


            def pe_xhT(pe, j):
                for h in range(2):
                    pe.wait_ge(xh_ok, 2 * j + h + 1)
                    for b in graphs(h):
                        last = nc.tensor.transpose(ps_t[h][:, b % HALF, :], xh[:, b, :], ident[:])
                    last.then_inc(xhT_ps, 1)

            def pe_xnT(pe, j):
                for h in range(2):
                    pe.wait_ge(xn_ok, 2 * j + h + 1)
                    if from_octet(j, 3):
                        pe.wait_ge(xhT_ok, 2 * j + h - 5)
                    for b in graphs(h):
                        last = nc.tensor.transpose(ps_t[h][:, b % HALF, :], xn[:, b, :], ident[:])
                    last.then_inc(xnT_ps, 1)

            def pe_logits(pe, j):
                for h in range(2):
                    pe.wait_ge(xhT_ok, 2 * j + h + 1)
                    if h == 0 and from_octet(j, 1):
                        pe.wait_ge(rank_read, j)
                    for b in graphs(h):
                        last = nc.tensor.matmul(ps_m[:, 0, b * E:(b + 1) * E], xhT[:, b, :], wrs[:],
                                                start=True, stop=True)
                last.then_inc(lg_ps, 1)

            def pe_front(pe, j, h):
                pe.wait_ge(xnT_ok, 2 * j + h + 1)
                if from_octet(j, 1):
                    pe.wait_ge(u_read, 2 * j + h - 1)
                nc.tensor.matmul(ps_u[h][:], a2rep[:], xnT[:, half(h), :], start=True, stop=False)
                for b in graphs(h):
                    last = nc.tensor.matmul(ps_u[h][:, b % HALF, :], xnT[:, b, :], a1rep[:],
                                            start=False, stop=(b % HALF == HALF - 1))
                last.then_inc(u_ps, 1)
                if h or from_octet(j, 1):
                    pe.wait_ge(wh_ok, 2 * j + h)
                for b in graphs(h):
                    last = nc.tensor.matmul(ps_wh[:, b % HALF, :], xnT[:, b, :], gw[:], start=True, stop=True)
                last.then_inc(wh_ps, 1)

            def pe_prT(pe, j):
                for h in range(2):
                    pe.wait_ge(ex_ok, 2 * j + h + 1)
                    for b in graphs(h):
                        last = nc.tensor.transpose(ps_t[h][:, b % HALF, :], ex[:, b, :], ident[:])
                    last.then_inc(prT_ps, 1)

            def pe_attend(pe, j, r):
                for h in range(2):
                    pe.wait_ge(prT_ok, 2 * j + h + 1)
                    pe.wait_ge(wh_ok, 2 * j + h + 1)
                    if from_octet(j, 1):
                        pe.wait_ge(h_read, 2 * j + h - 1)
                    for b in graphs(h):
                        last = nc.tensor.matmul(ps_h[h][:, b % HALF, :], prT[:, b, :], wh[r][:, b, :],
                                                start=True, stop=True)
                    last.then_inc(h_ps, 1)

            def pe_ranks(pe, j):
                pe.wait_ge(both_ok, j + 1)
                rank = ps_m[:, 1, :]
                nc.tensor.matmul(rank, tri[:], both[:], start=True, stop=False)
                for s in range(1, OCT):
                    nc.tensor.matmul(rank[:, s * E:], ones[:], both[:, 0:OCT - s, :], start=False, stop=False)
                nc.tensor.matmul(rank.rearrange("p (b e) -> p b e", e=E), ones[:],
                                 taken[:].unsqueeze(1).to_broadcast([P, OCT, E]),
                                 start=False, stop=True).then_inc(rank_ps, 1)

            def act_xhT(act, j):
                for h in range(2):
                    act.wait_ge(xhT_ps, 2 * j + h + 1)
                    if h == 0 and from_octet(j, 1):
                        act.wait_ge(lg_ps, j)
                    nc.scalar.copy(xhT[:, half(h), :], ps_t[h][:]).then_inc(xhT_ok, 1)

            def act_xnT(act, j):
                for h in range(2):
                    act.wait_ge(xnT_ps, 2 * j + h + 1)
                    if from_octet(j, 1):
                        act.wait_ge(wh_ps, 2 * j + h - 1)
                    nc.scalar.copy(xnT[:, half(h), :], ps_t[h][:]).then_inc(xnT_ok, 1)

            def act_exp(act, j, h):
                act.wait_ge(nbig_ok, j + 1)
                act.wait_ge(e_ok, 2 * j + h + 1)
                for b in graphs(h):
                    last = nc.scalar.activation(ex[:, b, :], ex[:, b, :], ACT.Exp, bias=nbig[:, b:b + 1],
                                                accum_out=den[:, b:b + 1])
                last.then_inc(ex_ok, 1)

            def act_wh(act, j, r, h):
                act.wait_ge(wh_ps, 2 * j + h + 1)
                if from_octet(j, 2):
                    act.wait_ge(h_ps, 2 * j + h - 3)
                nc.scalar.copy(wh[r][:, half(h), :], ps_wh[:]).then_inc(wh_ok, 1)

            def act_prT(act, j):
                for h in range(2):
                    act.wait_ge(prT_ps, 2 * j + h + 1)
                    if from_octet(j, 1):
                        act.wait_ge(h_ps, 2 * j + h - 1)
                    nc.scalar.copy(prT[:, half(h), :], ps_t[h][:]).then_inc(prT_ok, 1)

            def act_stage(act, j, r, turn):
                act.wait_ge(xh_ok, 2 * j + 2)
                if from_octet(j, 2):
                    act.wait_ge(scattered[r], 16 * 2 * OCT * turn)
                for k in range(2):
                    nc.scalar.copy(stage[r][:, k, :, 0:D], xh[:]).then_inc(copied, 1)

            def act_gap(act, j):
                act.wait_ge(gap_ok, j + 1)
                nc.scalar.activation(egap[:], gap[:], ACT.Exp).then_inc(egap_ok, 1)

            def act_norm1(act, j):
                act.wait_ge(root1_ok, 2 * j + 2)
                for h in range(2):
                    if from_octet(j, 1):
                        act.wait_ge(xnT_ps, 2 * j + h - 1)
                    for b in graphs(h):
                        last = nc.scalar.activation(xn[:, b, :], tok[:, ds(j * OCT + b, 1), :].squeeze(1),
                                                    ACT.Identity, bias=shift1[:, b:b + 1], scale=root1[:, b:b + 1])
                    last.then_inc(xn_ok, 1)

            def pool_scatter(pool, j, r):
                wait_apart(pool, slots_ok, j + 1, passed_pool)
                for k in range(2):
                    for b in range(OCT):
                        nc.gpsimd.indirect_dma_start(
                            out=rows_dram, out_offset=bass.IndirectOffsetOnAxis(ap=slots[r][:, k, b:b + 1], axis=0),
                            in_=stage[r][:, k, b, :], in_offset=None).then_inc(scattered[r], 16)

            class Chain:

                def __init__(self, dve, step):
                    self.dve, self.step, self.n = dve, step, 0
                    dve.sem_clear(step)

                def mark(self, ins):
                    self.n += 1
                    ins.then_inc(self.step, 1)

                def follow(self):
                    self.dve.wait_ge(self.step, self.n)

            def alternate(*streams):
                streams = list(streams)
                while streams:
                    for stream in list(streams):
                        if next(stream, None) is None:
                            streams.remove(stream)

            def dve_scores(dve, j):
                chain = Chain(dve, score_step)
                if from_octet(j, 1):
                    dve.wait_ge(ex_ok, 2 * j)
                    chain.mark(nc.vector.reciprocal(rden[:], den[:]))
                for h in range(2):
                    wait_apart(dve, u_ps, 2 * j + h + 1, passed_dve)
                    for b in graphs(h):
                        last = nc.vector.tensor_tensor_reduce(out=um[:, b, :], in0=ps_u[h][:, b % HALF, :],
                                                              in1=mask[:], scale=1.0, scalar=LOWEST, op0=ALU.add,
                                                              op1=ALU.max, accum_out=top[:, b:b + 1])
                    last.then_inc(u_read, 1)
                dve.wait_ge(u_read, 2 * j + 2)
                chain.mark(nc.vector.tensor_scalar(ntop[:], top[:], -1.0, None, ALU.mult))
                for h in range(2):
                    if from_octet(j, 1):
                        dve.wait_ge(prT_ps, 2 * j + h - 1)
                    nc.vector.scalar_tensor_tensor(ex[:, half(h), :], um[:, half(h), :], SLOPE, um[:, half(h), :],
                                                   ALU.mult, ALU.max).then_inc(e_ok, 1)
                    if h == 0:
                        chain.follow()
                        nc.vector.scalar_tensor_tensor(nbig[:], ntop[:], SLOPE, ntop[:],
                                                       ALU.mult, ALU.min).then_inc(nbig_ok, 1)

            def dve_last_sums(dve, j):
                dve.wait_ge(ex_ok, 2 * j + 2)
                chain = Chain(dve, score_step)
                chain.mark(nc.vector.reciprocal(rden[:], den[:]))
                chain.follow()

            def dve_residual(dve, j):
                for h in range(2):
                    dve.wait_ge(h_ps, 2 * j + h + 1)
                    for b in graphs(h):
                        t = tok[:, ds(j * OCT + b, 1), :].squeeze(1)
                        last = nc.vector.scalar_tensor_tensor(t, ps_h[h][:, b % HALF, :], rden[:, b:b + 1], t,
                                                              ALU.mult, ALU.add)
                    last.then_inc(h_read, 1)

            def dve_moments2(dve, j):
                chain = Chain(dve, moment2_step)
                for h in range(2):
                    wait_apart(dve, h_read, 2 * j + h + 1, passed_dve)
                    for b in graphs(h):
                        chain.mark(nc.vector.bn_stats(bn2[:, b, :], tok[:, ds(j * OCT + b, 1), :]))
                for b in range(OCT):
                    dve.wait_ge(moment2_step, b + 1)
                    last = nc.vector.bn_aggr(mv2[:, b, :], bn2[:, b, :])
                chain.mark(last)
                chain.follow()

            def dve_moments1(dve, j, r):
                chain = Chain(dve, moment1_step)
                for b in range(OCT):
                    chain.mark(nc.vector.bn_stats(bn[:, b, :], tok[:, ds(j * OCT + b, 1), :]))
                    yield True
                for b in range(OCT):
                    dve.wait_ge(moment1_step, b + 1)
                    last = nc.vector.bn_aggr(mv[r][:, b, :], bn[:, b, :])
                    if b < OCT - 1:
                        yield True
                chain.mark(last)
                yield True
                chain.follow()

            def dve_roots(dve, one, r_one, two):
                chain = Chain(dve, root_step)
                if one is not None:
                    chain.mark(nc.vector.tensor_scalar(var[:, 0, :], mv[r_one][:, :, 1], EPS, None, ALU.add))
                    yield True
                if two is not None:
                    chain.mark(nc.vector.tensor_scalar(var[:, 1, :], mv2[:, :, 1], EPS, None, ALU.add))
                    yield True
                    chain.follow()
                    chain.mark(nc.vector.scalar_tensor_tensor(var[:, 2, :], var[:, 1, :], EPS, mv2[:, :, 1],
                                                              ALU.mult, ALU.add))
                    yield True
                n = slice(0 if one is not None else 1, 3 if two is not None else 1)
                chain.follow()
                chain.mark(nc.vector.tensor_scalar(seed[:, n, :].bitcast(I32), var[:, n, :].bitcast(I32),
                                                   -0.5, ROOT_SEED, ALU.mult, ALU.add))
                yield True
                src, dst = seed, root
                for _ in range(3):
                    chain.follow()
                    chain.mark(nc.vector.tensor_tensor(tiny[:, n, :], src[:, n, :], src[:, n, :], ALU.mult))
                    yield True
                    chain.follow()
                    chain.mark(nc.vector.scalar_tensor_tensor(tiny[:, n, :], tiny[:, n, :], -0.5, var[:, n, :],
                                                              ALU.mult, ALU.mult))
                    yield True
                    chain.follow()
                    chain.mark(nc.vector.scalar_tensor_tensor(dst[:, n, :], tiny[:, n, :], 1.5, src[:, n, :],
                                                              ALU.add, ALU.mult))
                    yield True
                    src, dst = dst, src
                chain.follow()
                if one is not None:
                    if from_octet(one, 1):
                        dve.wait_ge(xn_ok, 2 * one)
                    nc.vector.tensor_copy(root1[:], src[:, 0, :]).then_inc(root1_ok, 1)
                    yield True
                    nc.vector.scalar_tensor_tensor(shift1[:], mv[r_one][:, :, 0], -1.0, src[:, 0, :],
                                                   ALU.mult, ALU.mult).then_inc(root1_ok, 1)
                    yield True
                if two is not None:
                    chain.mark(nc.vector.tensor_tensor(tiny[:, 0, :], var[:, 2, :], src[:, 2, :], ALU.mult))
                    yield True
                    if from_octet(two, 1):
                        dve.wait_ge(lg_read, two)
                    chain.follow()
                    chain.mark(nc.vector.tensor_tensor(ratio[:], tiny[:, 0, :], src[:, 1, :], ALU.mult))
                    yield True
                    chain.follow()

            def dve_norm2(dve, j, h):
                if from_octet(j, 1):
                    dve.wait_ge(xhT_ps, 2 * j + h - 1)
                    dve.wait_ge(copied, 2 * j)
                for b in graphs(h):
                    last = nc.vector.tensor_scalar(xh[:, b, :], tok[:, ds(j * OCT + b, 1), :].squeeze(1),
                                                   mv2[:, b, 0:1], root[:, 2, b:b + 1], ALU.subtract, ALU.mult)
                    if b < (h + 1) * HALF - 1:
                        yield True
                last.then_inc(xh_ok, 1)
                yield True

            def wide(v):
                return v.unsqueeze(2).to_broadcast([P, OCT, E])

            def each(v):
                return v.unsqueeze(1).to_broadcast([P, OCT, E])

            def dve_choose(dve, j):
                chain = Chain(dve, choice_step)
                dve.wait_ge(lg_ps, j + 1)
                nc.vector.tensor_tensor(lg[:], ps_m[:, 0, :].rearrange("p (b e) -> p b e", e=E), wide(ratio[:]),
                                        ALU.mult).then_inc(lg_read, 1)
                yield True
                dve.wait_ge(lg_read, j + 1)
                chain.mark(nc.vector.tensor_tensor(lg[:], lg[:], each(brs[:]), ALU.add))
                yield True
                for k, src in enumerate((lg, lg2)):
                    chain.follow()
                    chain.mark(nc.vector.tensor_reduce(best[:, k, :], src[:], AX.X, ALU.max))
                    yield True
                    chain.follow()
                    chain.mark(nc.vector.tensor_tensor(eq[:], src[:], wide(best[:, k, :]), ALU.is_equal))
                    yield True
                    chain.follow()
                    chain.mark(nc.vector.tensor_tensor(eq[:], eq[:], each(ranked[:]), ALU.mult))
                    yield True
                    chain.follow()
                    chain.mark(nc.vector.tensor_reduce(pick[:], eq[:], AX.X, ALU.max))
                    yield True
                    chain.follow()
                    chain.mark(nc.vector.tensor_tensor(hot[:, k], wide(pick[:]), each(ranked[:]), ALU.is_equal))
                    yield True
                    chain.follow()
                    if k == 0:
                        chain.mark(nc.vector.scalar_tensor_tensor(lg2[:], hot[:, 0], LOWEST, lg[:],
                                                                  ALU.mult, ALU.add))
                        yield True
                nc.vector.tensor_tensor(both[:], hot[:, 0], hot[:, 1], ALU.add).then_inc(both_ok, 1)
                yield True
                nc.vector.tensor_tensor(gap[:], best[:, 1, :], best[:, 0, :], ALU.subtract).then_inc(gap_ok, 1)
                yield True

            def dve_place(dve, j, r):
                chain = Chain(dve, place_step)
                dve.wait_ge(copied, 2 * j + 2)
                chain.mark(nc.vector.tensor_copy(stage[r][:, :, :, D].bitcast(I32), ids[:, :, ds(j * OCT, OCT)]))
                yield True
                dve.wait_ge(egap_ok, j + 1)
                chain.mark(nc.vector.tensor_scalar(share[:], egap[:], 1.0, None, ALU.add))
                yield True
                chain.follow()
                chain.mark(nc.vector.reciprocal(stage[r][:, 0, :, D + 1], share[:]))
                yield True
                chain.follow()
                chain.mark(nc.vector.tensor_tensor(stage[r][:, 1, :, D + 1], egap[:], stage[r][:, 0, :, D + 1],
                                                   ALU.mult))
                yield True
                dve.wait_ge(rank_ps, j + 1)
                nc.vector.tensor_tensor(place[:], ps_m[:, 1, :].rearrange("p (b e) -> p b e", e=E),
                                        each(region[:]), ALU.add).then_inc(rank_read, 1)
                yield True
                dve.wait_ge(rank_read, j + 1)
                chain.mark(nc.vector.tensor_tensor(
                    chosen[:].rearrange("p k b e -> p k (b e)"), hot[:].rearrange("p k b e -> p k (b e)"),
                    place[:].rearrange("p b e -> p (b e)").unsqueeze(1).to_broadcast([P, 2, OCT * E]), ALU.mult))
                yield True
                chain.mark(nc.vector.tensor_reduce(new[:], both[:].rearrange("p b e -> p e b"), AX.X, ALU.add))
                chain.follow()
                with nc.allow_low_precision(reason="one term of each sum is not zero, a whole number below 2^24"):
                    nc.vector.tensor_reduce(slots[r][:], chosen[:], AX.X, ALU.add).then_inc(slots_ok, 1)
                yield True
                chain.mark(nc.vector.tensor_tensor(taken[:], taken[:], new[:], ALU.add))
                yield True
                chain.follow()


            def has(j):
                return not isinstance(j, int) or 0 <= j < NO

            def pe_iteration(pe, i, r):
                if has(i - 2):
                    pe_xhT(pe, i - 2)
                if has(i + 1):
                    pe_xnT(pe, i + 1)
                if has(i - 2):
                    pe_logits(pe, i - 2)
                if has(i + 1):
                    for h in range(2):
                        pe_front(pe, i + 1, h)
                if has(i):
                    pe_prT(pe, i)
                    pe_attend(pe, i, r)
                if has(i - 2):
                    pe_ranks(pe, i - 2)

            def act_iteration(act, i, r, turn):
                if has(i - 2):
                    act_xhT(act, i - 2)
                if has(i + 1):
                    act_xnT(act, i + 1)
                for h in range(2):
                    if has(i):
                        act_exp(act, i, h)
                    if has(i + 1):
                        act_wh(act, i + 1, 1 - r, h)
                if has(i):
                    act_prT(act, i)
                if has(i - 2):
                    act_stage(act, i - 2, r, turn)
                    act_gap(act, i - 2)
                if has(i + 2):
                    act_norm1(act, i + 2)

            def dve_iteration(dve, i, r):
                if has(i):
                    dve_scores(dve, i)
                elif has(i - 1):
                    dve_last_sums(dve, i - 1)
                if has(i - 1):
                    dve_residual(dve, i - 1)
                    dve_moments2(dve, i - 1)
                streams = []
                if has(i + 2) or has(i - 1):
                    streams.append(dve_roots(dve, i + 2 if has(i + 2) else None, r, i - 1 if has(i - 1) else None))
                if has(i - 2):
                    streams.append(dve_choose(dve, i - 2))
                if has(i + 3):
                    streams.append(dve_moments1(dve, i + 3, 1 - r))
                alternate(*streams)
                if has(i - 1):
                    alternate(dve_norm2(dve, i - 1, 0))
                streams = []
                if has(i - 1):
                    streams.append(dve_norm2(dve, i - 1, 1))
                if has(i - 2):
                    streams.append(dve_place(dve, i - 2, r))
                alternate(*streams)

            HEAD, TURNS = 4, (NO - 7) // 2
            REST = HEAD + 2 * TURNS

            def iterations(engine, iteration):
                for i in range(-3, HEAD):
                    iteration(i, i % 2, (i - 2) // 2)
                with engine.Fori(0, TURNS) as n:
                    for r in range(2):
                        iteration(2 * n + (HEAD + r), r, n + (HEAD - 2) // 2)
                for i in range(REST, NO + 2):
                    iteration(i, i % 2, (i - 2) // 2)

            with nc.Block() as block:
                @block.tensor
                def _(pe):
                    iterations(pe, lambda i, r, turn: pe_iteration(pe, i, r))

                @block.scalar
                def _(act):
                    iterations(act, lambda i, r, turn: act_iteration(act, i, r, turn))

                @block.gpsimd
                def _(pool):
                    def step_of(i, r, turn):
                        if has(i - 2):
                            pool_scatter(pool, i - 2, r)
                    iterations(pool, step_of)
                    for r in range(2):
                        pool.wait_ge(scattered[r], 16 * 2 * OCT * (NO // 2))

                @block.vector
                def _(dve):
                    iterations(dve, lambda i, r, turn: dve_iteration(dve, i, r))

        with ExitStack() as ctx:
            def sb(name, shape, dt=F32):
                return ctx.enter_context(nc.sbuf_tensor(name, shape, dt))

            def sem(name):
                return ctx.enter_context(nc.semaphore(name))

            KT = TOKENS // TILE
            count = sb("count", [1, E])
            fills = sb("fills_", [1, E, KT])
            kth = sb("kth", [1, KT])
            tiles = sb("tiles", [1, E])
            ends = sb("ends", [1, E])
            jth = sb("jth", [1, NT])
            past = sb("past", [1, NT, E])
            skip = sb("skip", [1, NT, E])
            who = sb("who", [1, NT])
            before = sb("before", [1, NT])
            rowf = sb("rowf", [1, NT])
            ps_n = ctx.enter_context(nc.psum_tensor("ps_n", [P, E], F32))

            count_ps = sem("count_ps")
            iotas = sem("iotas2")
            tails_ok = sem("tails_ok")
            table_ok = sem("table_ok")
            padded = sem("padded")
            step = sem("step2")

            with nc.Block() as block:
                @block.gpsimd
                def _(pool):
                    nc.gpsimd.iota(kth[:], pattern=[[TILE, KT]], base=0, channel_multiplier=0,
                                   allow_small_or_imprecise_dtypes=True).then_inc(iotas, 1)
                    nc.gpsimd.iota(jth[:], pattern=[[1, NT]], base=0, channel_multiplier=0,
                                   allow_small_or_imprecise_dtypes=True).then_inc(iotas, 1)

                @block.tensor
                def _(pe):
                    nc.tensor.matmul(ps_n[:], ones[:], taken[:], start=True, stop=True).then_inc(count_ps, 1)

                @block.sync
                def _(sp):
                    sp.wait_ge(tails_ok, 1)
                    for e in range(E):
                        row = sp.value_load(tails[0:1, e:e + 1], min_val=e * CAP, max_val=e * CAP + TOKENS)
                        sp.dma_start(rows_dram[bass.ds(row, TILE), :],
                                     pads_dram[e * TILE:(e + 1) * TILE, :]).then_inc(padded, 16)
                    sp.wait_ge(padded, 16 * E)

                @block.vector
                def _(dve):
                    steps = [0]

                    def link(ins):
                        steps[0] += 1
                        ins.then_inc(step, 1)
                        dve.wait_ge(step, steps[0])

                    dve.wait_ge(count_ps, 1)
                    link(nc.vector.tensor_copy(count[:], ps_n[0:1, :]))
                    nc.vector.tensor_tensor(tails[:], count[:], region[0:1, :], ALU.add).then_inc(tails_ok, 1)
                    dve.wait_ge(iotas, 2)
                    link(nc.vector.tensor_tensor(fills[:], count[:].unsqueeze(2).to_broadcast([1, E, KT]),
                                                 kth[:].unsqueeze(1).to_broadcast([1, E, KT]), ALU.is_gt))
                    link(nc.vector.tensor_reduce(tiles[:], fills[:], AX.X, ALU.add))
                    link(nc.vector.tensor_copy(ends[:, 0:1], tiles[:, 0:1]))
                    for e in range(1, E):
                        link(nc.vector.tensor_tensor(ends[:, e:e + 1], ends[:, e - 1:e], tiles[:, e:e + 1], ALU.add))
                    link(nc.vector.tensor_tensor(past[:], jth[:].unsqueeze(2).to_broadcast([1, NT, E]),
                                                 ends[:].unsqueeze(1).to_broadcast([1, NT, E]), ALU.is_ge))
                    link(nc.vector.tensor_reduce(who[:], past[:], AX.X, ALU.add))
                    link(nc.vector.tensor_tensor(skip[:], past[:], tiles[:].unsqueeze(1).to_broadcast([1, NT, E]),
                                                 ALU.mult))
                    link(nc.vector.tensor_reduce(before[:], skip[:], AX.X, ALU.add))
                    link(nc.vector.tensor_tensor(rowf[:], jth[:], before[:], ALU.subtract))
                    link(nc.vector.tensor_scalar(rowf[:], rowf[:], float(TILE), None, ALU.mult))
                    link(nc.vector.scalar_tensor_tensor(table[:, 0, :], who[:], float(CAP), rowf[:],
                                                        ALU.mult, ALU.add))
                    link(nc.vector.tensor_scalar(who[:], who[:], float(E - 1), None, ALU.min))
                    link(nc.vector.tensor_copy(table[:, 1, :], who[:]))
                    nc.vector.tensor_scalar(table[:, 2, :], who[:], float(HC + 1), None,
                                            ALU.mult).then_inc(table_ok, 1)
                    dve.wait_ge(table_ok, 1)

        before_experts.close()

        with ExitStack() as ctx:
            def sb(name, shape, dt=F32):
                return ctx.enter_context(nc.sbuf_tensor(name, shape, dt))

            def ps(name, shape):
                return ctx.enter_context(nc.psum_tensor(name, shape, F32))

            def sem(name):
                return ctx.enter_context(nc.semaphore(name))

            XB = 2
            xs = [sb(f"xs{n}", [P, CH, R]) for n in range(XB)]
            w1c = [sb(f"w1c{r}", [P, 2, H], F32R) for r in range(2)]
            w2c = [sb(f"w2c{r}", [P, 2, HC * D], F32R) for r in range(2)]
            xT = [sb(f"xT{r}", [P, 2, TILE], F32R) for r in range(2)]
            hf = [sb(f"hf{c}", [P, TILE]) for c in range(HC)]
            hs = [sb(f"hs{r}", [P, 2, HC, TILE], F32R) for r in range(2)]
            yT = sb("yT", [P, TILE])
            ys = [sb(f"ys{r}", [P, CH, D]) for r in range(2)]
            yid = [sb(f"yid{r}", [P, CH], I32) for r in range(2)]
            tile_id = [sb(f"tile_id{n}", [P, CH], I32) for n in range(4)]
            tile_wt = [sb(f"tile_wt{n}", [P, CH]) for n in range(4)]
            ps_x = ps("ps_x", [P, CH, P])
            ps_l1 = [ps(f"ps_l1_{c}", [P, TILE]) for c in range(HC)]
            ps_l2 = ps("ps_l2", [P, TILE])
            ps_y = ps("ps_y", [P, CH, D])

            x_in = [sem(f"x_in{r}") for r in range(XB)]
            w1_in = [sem(f"w1_in{r}") for r in range(2)]
            w2_in = [sem(f"w2_in{r}") for r in range(2)]
            x_ps = sem("x_ps")
            xhigh_ok = sem("xhigh_ok")
            xlow_ok = sem("xlow_ok")
            l1_ps = sem("l1_ps")
            gelu_ok = sem("gelu_ok")
            high_ok = sem("high_ok")
            acthigh_ok = sem("acthigh_ok")
            low_ok = sem("low_ok")
            l2_ps = sem("l2_ps")
            yT_ok = sem("yT_ok")
            y_ps = sem("y_ps")
            ys_ok = sem("ys_ok")
            tails_ok = sem("tails_kept")
            yid_ok = sem("yid_ok")
            passed = sem("passed")
            sent = [sem(f"sent{r}") for r in range(2)]


            def pe_x(pe, t, q, turn):
                pe.wait_ge(x_in[q % 2], 32 * turn + 16 * (q // 2) + 16)
                if not isinstance(t, int) or t >= 1:
                    pe.wait_ge(xlow_ok, t)
                for c in range(CH):
                    last = nc.tensor.transpose(ps_x[:, c, :], xs[q % 2][:, c, 0:D], ident[:])
                last.then_inc(x_ps, 1)

            def pe_layer1(pe, t, q, turn, c):
                r = q % 2
                if c == 0:
                    pe.wait_ge(w1_in[r], 32 * turn + 16 * (q // 2) + 16)
                    pe.wait_ge(xlow_ok, t + 1)
                if not isinstance(t, int) or t >= 1:
                    pe.wait_ge(gelu_ok, HC * t + c - HC + 1)
                for n, (a, b) in enumerate(((0, 0), (0, 1), (1, 0))):
                    last = nc.tensor.matmul(ps_l1[c][:], w1c[r][:, a, c * P:(c + 1) * P], xT[r][:, b, :],
                                            start=(n == 0), stop=(n == 2))
                last.then_inc(l1_ps, 1)

            def pe_layer2(pe, t, q, turn):
                r = q % 2
                pe.wait_ge(w2_in[r], 32 * turn + 16 * (q // 2) + 16)
                if not isinstance(t, int) or t >= 1:
                    pe.wait_ge(yT_ok, t)
                for c in range(HC):
                    pe.wait_ge(low_ok, HC * t + c + 1)
                    for n, (a, b) in enumerate(((0, 0), (0, 1), (1, 0))):
                        last = nc.tensor.matmul(ps_l2[:], w2c[r][:, a, c * D:(c + 1) * D], hs[r][:, b, c, :],
                                                start=(c == 0 and n == 0), stop=(c == HC - 1 and n == 2))
                last.then_inc(l2_ps, 1)

            def pe_y(pe, t):
                pe.wait_ge(yT_ok, t + 1)
                if not isinstance(t, int) or t >= 1:
                    pe.wait_ge(ys_ok, t)
                for c in range(CH):
                    last = nc.tensor.transpose(ps_y[:, c, :], yT[:, c * P:(c + 1) * P], ident[:])
                last.then_inc(y_ps, 1)

            def act_x(act, t, q):
                act.wait_ge(x_ps, t + 1)
                if not isinstance(t, int) or t >= 2:
                    act.wait_ge(l1_ps, HC * t - HC)
                nc.scalar.copy(xT[q % 2][:, 0, :], ps_x[:].rearrange("p c n -> p (c n)")).then_inc(xhigh_ok, 1)

            def act_gelu(act, t, c, column):
                act.wait_ge(l1_ps, HC * t + c + 1)
                if not isinstance(t, int) or t >= 1:
                    act.wait_ge(low_ok, HC * t + c - HC + 1)
                nc.scalar.activation(hf[c][:], ps_l1[c][:], ACT.Gelu,
                                     bias=biases[:, ds(column + c, 1)]).then_inc(gelu_ok, 1)

            def act_high(act, t, q, c):
                act.wait_ge(gelu_ok, HC * t + c + 1)
                if not isinstance(t, int) or t >= 2:
                    act.wait_ge(l2_ps, t - 1)
                nc.scalar.copy(hs[q % 2][:, 0, c, :], hf[c][:]).then_inc(acthigh_ok, 1)

            def act_y(act, t, column):
                act.wait_ge(l2_ps, t + 1)
                if not isinstance(t, int) or t >= 1:
                    act.wait_ge(y_ps, t)
                nc.scalar.activation(yT[:], ps_l2[:], ACT.Identity,
                                     bias=biases[:, ds(column + HC, 1)]).then_inc(yT_ok, 1)

            def dve_x(dve, t, q, turn):
                dve.wait_ge(x_in[q % 2], 32 * turn + 16 * (q // 2) + 16)
                if not isinstance(t, int) or t >= 4:
                    dve.wait_ge(ys_ok, t - 3)
                nc.vector.tensor_copy(tile_id[q][:], xs[q % 2][:, :, D].bitcast(I32)).then_inc(tails_ok, 1)
                nc.vector.tensor_copy(tile_wt[q][:], xs[q % 2][:, :, D + 1]).then_inc(tails_ok, 1)
                dve.wait_ge(xhigh_ok, t + 1)
                if not isinstance(t, int) or t >= 2:
                    dve.wait_ge(l1_ps, HC * t - HC)
                nc.vector.tensor_tensor(xT[q % 2][:, 1, :], ps_x[:].rearrange("p c n -> p (c n)"),
                                        xT[q % 2][:, 0, :].bitcast(F32), ALU.subtract).then_inc(xlow_ok, 1)

            def dve_high(dve, t, q, c):
                dve.wait_ge(gelu_ok, HC * t + c + 1)
                if not isinstance(t, int) or t >= 2:
                    dve.wait_ge(l2_ps, t - 1)
                nc.vector.tensor_copy(hs[q % 2][:, 0, c, :], hf[c][:]).then_inc(high_ok, 1)

            def dve_low(dve, t, q, c):
                if c % 2:
                    dve.wait_ge(acthigh_ok, HC // 2 * t + c // 2 + 1)
                else:
                    dve.wait_ge(high_ok, HC // 2 * t + c // 2 + 1)
                nc.vector.tensor_tensor(hs[q % 2][:, 1, c, :], hf[c][:], hs[q % 2][:, 0, c, :].bitcast(F32),
                                        ALU.subtract).then_inc(low_ok, 1)

            def dve_y(dve, t, q, turn):
                r = q % 2
                dve.wait_ge(y_ps, t + 1)
                if not isinstance(t, int) or t >= 2:
                    dve.wait_ge(sent[r], 16 * CH * 2 * turn + 16 * CH * (q // 2))
                dve.wait_ge(tails_ok, 2 * t + 2)
                nc.vector.tensor_copy(yid[r][:], tile_id[q][:]).then_inc(yid_ok, 1)
                nc.vector.tensor_tensor(ys[r][:], ps_y[:], tile_wt[q][:].unsqueeze(2).to_broadcast([P, CH, D]),
                                        ALU.mult).then_inc(ys_ok, 1)

            def pool_y(pool, t, q):
                wait_apart(pool, ys_ok, t + 1, passed)
                wait_apart(pool, yid_ok, t + 1, passed)
                for c in range(CH):
                    nc.gpsimd.indirect_dma_start(
                        out=y_dram, out_offset=bass.IndirectOffsetOnAxis(ap=yid[q % 2][:, c:c + 1], axis=0),
                        in_=ys[q % 2][:, c, :], in_offset=None).then_inc(sent[q % 2], 16)

            def sp_x(sp, t, q):
                row = sp.value_load(table[0:1, 0, ds(t, 1)], min_val=0, max_val=E * CAP + (DEAD - 1) * TILE)
                if not isinstance(t, int) or t >= XB:
                    sp.wait_ge(x_ps, t - XB + 1)
                    sp.wait_ge(tails_ok, 2 * (t - XB) + 2)
                sp.dma_start(xs[q % 2][:], rows_dram[bass.ds(row, TILE), :].rearrange("(c p) r -> p c r", p=P)
                             ).then_inc(x_in[q % 2], 16)

            def sp_w1(sp, t, q):
                e = sp.value_load(table[0:1, 1, ds(t, 1)], min_val=0, max_val=E - 1)
                if not isinstance(t, int) or t >= 2:
                    sp.wait_ge(l1_ps, HC * t - HC)
                sp.dma_start(w1c[q % 2][:].rearrange("p a h -> p (a h)").bitcast(F32),
                             w1all[:, bass.ds(e * (2 * H), 2 * H)]).then_inc(w1_in[q % 2], 16)

            def sp_w2(sp, t, q):
                e = sp.value_load(table[0:1, 1, ds(t, 1)], min_val=0, max_val=E - 1)
                if not isinstance(t, int) or t >= 2:
                    sp.wait_ge(l2_ps, t - 1)
                sp.dma_start(w2c[q % 2][:].rearrange("p a h -> p (a h)").bitcast(F32),
                             w2all[:, bass.ds(e * (2 * HC * D), 2 * HC * D)]).then_inc(w2_in[q % 2], 16)

            biases = bias[:].rearrange("p e c -> p (e c)")
            w1all = w1s[:].rearrange("p e a h -> p (e a h)").bitcast(F32)
            w2all = w2s[:].rearrange("p e a h -> p (e a h)").bitcast(F32)

            HEAD = 3
            LOOPS = (NT - HEAD - 1) // 4
            REST = HEAD + 4 * LOOPS

            def previous(q, turn, n):
                return (q - n) % 4, turn + (q - n) // 4

            def iterations(engine, step_of):
                for t in range(HEAD):
                    step_of(t, t % 4, t // 4)
                with engine.Fori(0, LOOPS) as n:
                    for k in range(4):
                        step_of(4 * n + (HEAD + k), (HEAD + k) % 4, n + (HEAD + k) // 4)
                for t in range(REST, NT + 2):
                    step_of(t, t % 4, t // 4)

            def present(t, low, high=NT):
                return not isinstance(t, int) or low <= t < high

            with nc.Block() as block:
                @block.gpsimd
                def _(pool):
                    def step_of(t, q, turn):
                        if present(t, 2, NT + 2):
                            pool_y(pool, t - 2, (q - 2) % 4)
                    iterations(pool, step_of)
                    for r in range(2):
                        pool.wait_ge(sent[r], 16 * CH * ((NT - r + 1) // 2))

                @block.sync
                def _(sp):
                    sp_x(sp, 0, 0)
                    sp_w1(sp, 0, 0)
                    sp_x(sp, 1, 1)
                    sp_w1(sp, 1, 1)
                    sp_w2(sp, 0, 0)

                    def step_of(t, q, turn):
                        if present(t, 0, NT - 2):
                            sp_x(sp, t + 2, (q + 2) % 4)
                            sp_w1(sp, t + 2, (q + 2) % 4)
                        if present(t, 0, NT - 1):
                            sp_w2(sp, t + 1, (q + 1) % 4)
                    iterations(sp, step_of)

                @block.tensor
                def _(pe):
                    pe_x(pe, 0, 0, 0)

                    def step_of(t, q, turn):
                        if present(t, 0):
                            pe_layer1(pe, t, q, turn, 0)
                            pe_layer1(pe, t, q, turn, 1)
                        if present(t, 0, NT - 1):
                            pe_x(pe, t + 1, (q + 1) % 4, turn + (q + 1) // 4)
                        if present(t, 0):
                            pe_layer1(pe, t, q, turn, 2)
                            pe_layer1(pe, t, q, turn, 3)
                        if present(t, 2, NT + 2):
                            pe_y(pe, t - 2)
                        if present(t, 1, NT + 1):
                            pe_layer2(pe, t - 1, *previous(q, turn, 1))
                    iterations(pe, step_of)

                @block.scalar
                def _(act):
                    act_x(act, 0, 0)

                    def step_of(t, q, turn):
                        if present(t, 2, NT + 2):
                            column = act.value_load(table[0:1, 2, ds(t - 2, 1)], min_val=0, max_val=(E - 1) * (HC + 1))
                            act_y(act, t - 2, column)
                        if present(t, 0):
                            column = act.value_load(table[0:1, 2, ds(t, 1)], min_val=0, max_val=(E - 1) * (HC + 1))
                            act_gelu(act, t, 0, column)
                            act_gelu(act, t, 1, column)
                            act_high(act, t, q, 1)
                        if present(t, 0, NT - 1):
                            act_x(act, t + 1, (q + 1) % 4)
                        if present(t, 0):
                            act_gelu(act, t, 2, column)
                            act_gelu(act, t, 3, column)
                            act_high(act, t, q, 3)
                    iterations(act, step_of)

                @block.vector
                def _(dve):
                    dve_x(dve, 0, 0, 0)

                    def step_of(t, q, turn):
                        if present(t, 0):
                            dve_high(dve, t, q, 0)
                            dve_low(dve, t, q, 0)
                            dve_low(dve, t, q, 1)
                        if present(t, 0, NT - 1):
                            dve_x(dve, t + 1, (q + 1) % 4, turn + (q + 1) // 4)
                        if present(t, 0):
                            dve_high(dve, t, q, 2)
                            dve_low(dve, t, q, 2)
                        if present(t, 2, NT + 2):
                            dve_y(dve, t - 2, *previous(q, turn, 2))
                        if present(t, 0):
                            dve_low(dve, t, q, 3)
                    iterations(dve, step_of)

        with ExitStack() as ctx:
            YB = 4
            yb = [ctx.enter_context(nc.sbuf_tensor(f"yb{n}", [P, OCT, 2, D], F32)) for n in range(YB)]
            y_in = [ctx.enter_context(nc.semaphore(f"y_in{n}")) for n in range(YB)]
            summed = ctx.enter_context(nc.semaphore("summed"))
            total = ctx.enter_context(nc.semaphore("total"))
            stored = ctx.enter_context(nc.semaphore("stored"))
            y_tokens = y_dram[0:ROWS, :].rearrange("(g p k) d -> p g k d", p=P, k=2)

            with nc.Block() as block:
                @block.sync
                def _(sp):
                    for o in range(NO):
                        if o >= YB:
                            sp.wait_ge(total, o - YB + 1)
                        sp.dma_start(yb[o % YB][:], y_tokens[:, o * OCT:(o + 1) * OCT]).then_inc(y_in[o % YB], 16)

                @block.vector
                def _(dve):
                    for o in range(NO):
                        g = slice(o * OCT, (o + 1) * OCT)
                        dve.wait_ge(y_in[o % YB], 16 * (o // YB + 1))
                        nc.vector.tensor_tensor(tok[:, g, :], tok[:, g, :], yb[o % YB][:, :, 0, :],
                                                ALU.add).then_inc(summed, 1)
                        dve.wait_ge(summed, o + 1)
                        nc.vector.tensor_tensor(tok[:, g, :], tok[:, g, :], yb[o % YB][:, :, 1, :],
                                                ALU.add).then_inc(total, 1)

                @block.scalar
                def _(act):
                    for o in range(NO):
                        g = slice(o * OCT, (o + 1) * OCT)
                        act.wait_ge(total, o + 1)
                        act.dma_start(out[g].rearrange("g p d -> p g d"), tok[:, g, :]).then_inc(stored, 16)
                    act.wait_ge(stored, 16 * NO)


_INS = ["x", "adj", "L0_gnn_W", "L0_gnn_a", "L0_ffn_Wr", "L0_ffn_br", "L0_ffn_ln_g", "L0_ffn_ln_b",
        "L0_ffn_W1", "L0_ffn_b1", "L0_ffn_W2", "L0_ffn_b2"]


def kernel(**inputs):
    import numpy as np
    import concourse.bacc as bacc
    from concourse.bass_utils import run_bass_kernel_spmd

    nc = bacc.Bacc("TRN2", target_bir_lowering=False, num_devices=1)
    arrays, args = {}, []
    for name in _INS:
        a = np.ascontiguousarray(inputs[name])
        arrays[f"in_{name}"] = a
        args.append(nc.dram_tensor(f"in_{name}", a.shape, mybir.dt.from_np(a.dtype), kind="ExternalInput").ap())
    shape = inputs["x"].shape
    out = nc.dram_tensor("out_0", shape, F32, kind="ExternalOutput").ap()
    moe_kernel(nc, *args, out)
    r = run_bass_kernel_spmd(nc, [arrays], core_ids=[0])
    return r.results[0]["out_0"]
```

```python
from contextlib import ExitStack

import concourse.bass as bass
from concourse import mybir

F32 = mybir.dt.float32
F32R = mybir.dt.float32r
BF16 = mybir.dt.bfloat16
I32 = mybir.dt.int32
ALU = mybir.AluOpType
ACT = mybir.ActivationFunctionType
AX = mybir.AxisListType

P = 128
OCT = 8
HALF = OCT // 2
TILE = 512
CH = TILE // P
EPS = 1e-5
SLOPE = 0.2
MASKED = -1e30
LOWEST = -3e38
WHOLE = float(2 ** 23)
ROOT_SEED = float(0x5f375980)


def moe_kernel(nc, x, adj, gnn_w, gnn_a, wr, br, ln_g, ln_b, w1, b1, w2, b2, out):
    G, N, D = x.shape
    E, _, H = w1.shape
    HC = H // P
    NO = G // OCT
    TOKENS = G * N
    ROWS = 2 * TOKENS
    NT = ROWS // TILE + E - 1
    NE = NT + 1
    CAP = TOKENS + TILE
    R = D + 2
    FIRST = 4
    assert N == P and D == P and G % OCT == 0 and H % P == 0 and ROWS % TILE == 0 and NE % 2 == 0

    rows_dram = nc.dram_tensor("expert_rows", [E * CAP + 2 * TILE, R], F32).ap()
    pads_dram = nc.dram_tensor("pad_rows", [TILE, R], F32).ap()
    acc_dram = nc.dram_tensor("sums", [TOKENS + 3 * TILE, D], F32).ap()

    def wait_apart(engine, sem, value, passed):
        engine.wait_ge(sem, value)
        if not isinstance(value, int):
            engine.sem_inc(passed, 1)

    def ds(start, size):
        return slice(start, start + size) if isinstance(start, int) else bass.ds(start, size)

    with ExitStack() as whole:
        def keep(name, shape, dt=F32):
            return whole.enter_context(nc.sbuf_tensor(name, shape, dt))

        w1s = keep("w1s", [P, E, 2, H], F32R)
        w2s = keep("w2s", [P, E, 2, HC * D], F32R)
        bias = keep("bias", [P, E, HC + 1])
        ident = keep("ident", [P, P])
        table = keep("table", [1, 7, NE], I32)

        stage = [keep(f"stage{r}", [P, 2, OCT, R]) for r in range(2)]
        slots = [keep(f"slots{r}", [P, 2, OCT], I32) for r in range(2)]
        scattered = [whole.enter_context(nc.semaphore(f"scattered{r}")) for r in range(2)]

        w1c = [keep(f"w1c{r}", [P, 2, H], F32R) for r in range(2)]
        w2c = [keep("w2c0", [P, 2, HC * D], F32R)]
        w1_in = [whole.enter_context(nc.semaphore(f"w1_in{r}")) for r in range(2)]
        w2_in = [whole.enter_context(nc.semaphore(f"w2_in{r}")) for r in range(2)]
        w1all = w1s[:].rearrange("p e a h -> p (e a h)").bitcast(F32)
        w2all = w2s[:].rearrange("p e a h -> p (e a h)").bitcast(F32)

        def load_weights(sp, expert, r, buffers, source, width, arrived):
            sp.dma_start(buffers[r][:].rearrange("p a h -> p (a h)").bitcast(F32),
                         source[:, bass.ds(expert * width, width)]).then_inc(arrived[r], 16)

        def scatter_rows(r):
            for k in range(2):
                for b in range(OCT):
                    nc.gpsimd.indirect_dma_start(
                        out=rows_dram, out_offset=bass.IndirectOffsetOnAxis(ap=slots[r][:, k, b:b + 1], axis=0),
                        in_=stage[r][:, k, b, :], in_offset=None).then_inc(scattered[r], 16)

        to_route = whole.enter_context(ExitStack())

        def keep_to_route(name, shape, dt=F32):
            return to_route.enter_context(nc.sbuf_tensor(name, shape, dt))

        tok = keep_to_route("tok", [P, G, D])
        tri = keep_to_route("tri", [P, P], BF16)
        ones = keep_to_route("ones", [P, P], BF16)
        gw = keep_to_route("gw", [P, D])
        a1rep = keep_to_route("a1rep", [P, P])
        a2rep = keep_to_route("a2rep", [P, P])
        mask = keep_to_route("mask", [P, P])
        wrs = keep_to_route("wrs", [P, E])
        brs = keep_to_route("brs", [P, E])
        ranked = keep_to_route("ranked", [P, E])
        region = keep_to_route("region", [P, E])
        ids = keep_to_route("ids", [P, G], I32)
        kth = keep_to_route("kth", [1, TOKENS // TILE])
        jth = keep_to_route("jth", [1, NE])
        odd = keep_to_route("odd", [1, NE])
        taken = keep_to_route("taken", [P, E], BF16)
        tails = keep_to_route("tails", [1, E], I32)

        first_of_part = [0, 1, 3, 7]
        parts = [o * OCT for o in first_of_part] + [G]
        tok_in = [whole.enter_context(nc.semaphore(f"tok_in{n}")) for n in range(4)]
        raw1_in = [whole.enter_context(nc.semaphore(f"raw1_in{n}")) for n in range(E // 2)]
        raw2_in = [whole.enter_context(nc.semaphore(f"raw2_in{n}")) for n in range(E // 2)]
        NV = E * HC + 3 * E
        B2, LG, LB = E * HC, E * HC + E, E * HC + 2 * E
        vecs = keep_to_route("vecs", [NV, P])
        cols = keep_to_route("cols", [P, NV])
        pads = tok[:].rearrange("p g d -> p (g d)")[:, G * D - 3 * CH * R:].rearrange(
            "p (n c r) -> p n c r", c=CH, r=R)
        pads_out = whole.enter_context(nc.semaphore("pads_out"))
        vecs_in = whole.enter_context(nc.semaphore("vecs_in"))
        raw1 = w1s[:, :, 1, :].bitcast(F32)
        raw2 = w2s[:, :, 1, :].bitcast(F32)

        with ExitStack() as ctx:
            def sb(name, shape, dt=F32):
                return ctx.enter_context(nc.sbuf_tensor(name, shape, dt))

            def sem(name):
                return ctx.enter_context(nc.semaphore(name))

            adjs = sb("adjs", [P, P])
            arow = sb("arow", [P, 2, D])
            prod = sb("prod", [P, 2, D])
            acol = sb("acol", [P, 2])

            small_in = sem("small_in")
            fills = sem("fills")
            iotas = sem("iotas")
            pads_zero = sem("pads_zero")
            pads_ok = sem("pads_ok")
            acols = sem("acols")
            areps = sem("areps")

            with nc.Block() as block:
                @block.sync
                def _(sp):
                    sp.dma_start(adjs[:], adj).then_inc(small_in, 16)
                    for k in range(2):
                        a_k = gnn_a[k * D:(k + 1) * D, :].rearrange("d o -> (d o)")
                        sp.dma_start(arow[:, k, :], a_k.partition_broadcast(P)).then_inc(small_in, 16)

                @block.scalar
                def _(act):
                    act.dma_start(gw[:], gnn_w).then_inc(small_in, 16)
                    act.dma_start(tok[:, parts[0]:parts[1], :],
                                  x[parts[0]:parts[1]].rearrange("g p d -> p g d")).then_inc(tok_in[0], 16)
                    act.dma_start(wrs[:], wr).then_inc(small_in, 16)
                    act.dma_start(brs[:], br.partition_broadcast(P)).then_inc(small_in, 16)
                    act.wait_ge(pads_ok, 1)
                    act.dma_start(pads_dram.rearrange("(c p) r -> p c r", p=P), pads[:, 0]).then_inc(pads_out, 16)
                    act.dma_start(rows_dram[E * CAP:, :].rearrange("(n c p) r -> p n c r", p=P, c=CH),
                                  pads[:, 1:3]).then_inc(pads_out, 16)
                    act.dma_start(acc_dram[TOKENS:, :].rearrange("(n c p) d -> p n c d", p=P, c=CH),
                                  pads[:, :, :, 0:D]).then_inc(pads_out, 16)

                @block.gpsimd
                def _(pool):
                    nc.gpsimd.memset(pads, 0.0).then_inc(pads_zero, 1)
                    nc.gpsimd.memset(ident[:], 0.0).then_inc(fills, 1)
                    nc.gpsimd.memset(tri[:], 1.0).then_inc(fills, 1)
                    pool.wait_ge(pads_zero, 1)
                    nc.gpsimd.iota(pads[:, :, :, D:D + 1].bitcast(I32), pattern=[[TILE, 3], [P, CH], [1, 1]], base=TOKENS,
                                   channel_multiplier=1).then_inc(pads_ok, 1)
                    pool.wait_ge(fills, 2)
                    nc.gpsimd.affine_select(out=ident[:], in_=ident[:], compare_op=ALU.not_equal, fill=1.0, base=0,
                                            pattern=[[-1, P]], channel_multiplier=1).then_inc(iotas, 1)
                    nc.gpsimd.affine_select(out=tri[:], in_=tri[:], compare_op=ALU.is_gt, fill=0.0, base=0,
                                            pattern=[[1, P]], channel_multiplier=-1).then_inc(iotas, 1)
                    nc.gpsimd.iota(ids[:], pattern=[[N, G]], base=0, channel_multiplier=1).then_inc(iotas, 1)
                    nc.gpsimd.iota(kth[:], pattern=[[TILE, TOKENS // TILE]], base=0, channel_multiplier=0,
                                   allow_small_or_imprecise_dtypes=True).then_inc(iotas, 1)
                    nc.gpsimd.iota(jth[:], pattern=[[1, NE]], base=0, channel_multiplier=0,
                                   allow_small_or_imprecise_dtypes=True).then_inc(iotas, 1)
                    nc.gpsimd.iota(odd[:].rearrange("o (a b) -> o a b", b=2), pattern=[[0, NE // 2], [1, 2]], base=0,
                                   channel_multiplier=0, allow_small_or_imprecise_dtypes=True).then_inc(iotas, 1)
                    nc.gpsimd.iota(ranked[:], pattern=[[-1, E]], base=E, channel_multiplier=0,
                                   allow_small_or_imprecise_dtypes=True).then_inc(iotas, 1)
                    nc.gpsimd.iota(region[:], pattern=[[CAP, E]], base=0, channel_multiplier=0,
                                   allow_small_or_imprecise_dtypes=True).then_inc(iotas, 1)
                    pool.wait_ge(iotas, 8)

                @block.vector
                def _(dve):
                    nc.vector.memset(ones[:], 1.0)
                    nc.vector.memset(taken[:], 0.0)
                    dve.wait_ge(small_in, 96)
                    nc.vector.tensor_scalar(mask[:], adjs[:], 0.0, MASKED, ALU.is_equal, ALU.mult)
                    for k in range(2):
                        nc.vector.tensor_tensor_reduce(out=prod[:, k, :], in0=gw[:], in1=arow[:, k, :], scale=1.0,
                                                       scalar=0.0, op0=ALU.mult, op1=ALU.add,
                                                       accum_out=acol[:, k:k + 1]).then_inc(acols, 1)
                    for k, to in enumerate((a1rep, a2rep)):
                        dve.wait_ge(acols, k + 1)
                        nc.vector.tensor_copy(to[:], acol[:, k:k + 1].to_broadcast([P, P])).then_inc(areps, 1)
                    dve.wait_ge(areps, 2)

        with ExitStack() as ctx:
            def sb(name, shape, dt=F32):
                return ctx.enter_context(nc.sbuf_tensor(name, shape, dt))

            def ps(name, shape):
                return ctx.enter_context(nc.psum_tensor(name, shape, F32))

            def sem(name):
                return ctx.enter_context(nc.semaphore(name))

            xn = sb("xn", [P, OCT, D])
            xnT = sb("xnT", [P, OCT, P])
            wh = [sb(f"wh{r}", [P, OCT, D]) for r in range(2)]
            um = sb("um", [P, OCT, P])
            ex = sb("ex", [P, OCT, P])
            prT = sb("prT", [P, OCT, P])
            xh = sb("xh", [P, OCT, D])
            xhT = sb("xhT", [P, OCT, P])
            bn = sb("bn", [P, OCT, 6])
            mv = [sb(f"mv{r}", [P, OCT, 2]) for r in range(2)]
            bn2 = sb("bn2", [P, OCT, 6])
            mv2 = sb("mv2", [P, OCT, 2])
            var = sb("var", [P, 3, OCT])
            tiny = sb("tiny", [P, 3, OCT])
            seed = sb("seed", [P, 3, OCT])
            root = sb("root", [P, 3, OCT])
            shift1 = sb("shift1", [P, OCT])
            root1 = sb("root1", [P, OCT])
            shift2 = sb("shift2", [P, HALF])
            root2 = sb("root2", [P, HALF])
            ratio = sb("ratio", [P, OCT])
            top = sb("top", [P, OCT])
            ntop = sb("ntop", [P, OCT])
            nbig = sb("nbig", [P, OCT])
            den = sb("den", [P, OCT])
            rden = sb("rden", [P, OCT])
            lg = sb("lg", [P, OCT, E])
            lg2 = sb("lg2", [P, OCT, E])
            eq = sb("eq", [P, OCT, E])
            hot = sb("hot", [P, 2, OCT, E])
            best = sb("best", [P, 2, OCT])
            pick = sb("pick", [P, OCT])
            both = sb("both", [P, OCT, E], BF16)
            place = sb("place", [P, OCT, E])
            chosen = sb("chosen", [P, 2, OCT, E])
            gap = sb("gap", [P, OCT])
            egap = sb("egap", [P, OCT])
            share = sb("share", [P, OCT])
            new = sb("new", [P, E])

            ps_t = [ps(f"ps_t{h}", [P, HALF, P]) for h in range(2)]
            ps_wh = ps("ps_wh", [P, HALF, D])
            ps_u = [ps(f"ps_u{h}", [P, HALF, P]) for h in range(2)]
            ps_h = [ps(f"ps_h{h}", [P, HALF, D]) for h in range(2)]
            ps_m = ps("ps_m", [P, 2, OCT * E])

            root1_ok = sem("root1_ok")
            xn_ok = sem("xn_ok")
            xnT_ps = sem("xnT_ps")
            xnT_ok = sem("xnT_ok")
            wh_ps = sem("wh_ps")
            wh_ok = sem("wh_ok")
            u_ps = sem("u_ps")
            u_read = sem("u_read")
            nbig_ok = sem("nbig_ok")
            e_ok = sem("e_ok")
            ex_ok = sem("ex_ok")
            prT_ps = sem("prT_ps")
            prT_ok = sem("prT_ok")
            h_ps = sem("h_ps")
            h_read = sem("h_read")
            root2_ok = sem("root2_ok")
            xh_ok = sem("xh_ok")
            xh2_ok = sem("xh2_ok")
            copied = sem("copied")
            passed_dve = sem("passed_dve")
            passed_pool = sem("passed_pool")
            xhT_ps = sem("xhT_ps")
            xhT_ok = sem("xhT_ok")
            lg_ps = sem("lg_ps")
            lg_read = sem("lg_read")
            gap_ok = sem("gap_ok")
            egap_ok = sem("egap_ok")
            both_ok = sem("both_ok")
            rank_ps = sem("rank_ps")
            rank_read = sem("rank_read")
            slots_ok = sem("slots_ok")
            score_step = sem("score_step")
            moment1_step = sem("moment1_step")
            moment2_step = sem("moment2_step")
            root_step = sem("root_step")
            choice_step = sem("choice_step")
            place_step = sem("place_step")
            plan_step = sem("plan_step")
            cols_ps = sem("cols_ps")
            cols_ok = sem("cols_ok")
            b1_ps = sem("b1_ps")
            bias_ok = sem("bias_ok")
            high1 = sem("high1")
            low1 = sem("low1")
            high2 = sem("high2")
            low2 = sem("low2")
            stored = sem("stored")
            all_taken = sem("all_taken")
            count_ps = sem("count_ps")
            tails_ok = sem("tails_ok")
            table_ok = sem("table_ok")
            padded = sem("padded")

            KT = TOKENS // TILE
            count = sb("count", [1, 2, E])
            early = sb("early", [P, E], BF16)
            sooner = sb("sooner", [1, FIRST, E])
            reach = sb("reach", [1, FIRST])
            tiles = sb("tiles", [1, E])
            ends = sb("ends", [1, E])
            spare = um[0:1].rearrange("o b n -> o (b n)")
            fills = spare[:, 0:E * KT].rearrange("o (e k) -> o e k", k=KT)
            past = spare[:, E * KT:E * KT + NE * E].rearrange("o (t e) -> o t e", e=E)
            who = sb("who", [1, NE])
            before = sb("before", [1, NE])
            pairs = sb("pairs", [1, NE])
            rowf = sb("rowf", [1, NE])
            live = sb("live", [1, NE])

            def half(h):
                return slice(h * HALF, (h + 1) * HALF)

            def graphs(h):
                return range(h * HALF, (h + 1) * HALF)

            def from_octet(j, first):
                return not isinstance(j, int) or j >= first


            def pe_xhT(pe, j):
                for h in range(2):
                    pe.wait_ge((xh_ok, xh2_ok)[h], j + 1)
                    if has(j + 3):
                        pe.wait_ge(xnT_ok, 2 * j + h + 7)
                    elif has(j + 1):
                        pe.wait_ge(prT_ok, 2 * j + h + 3)
                    for b in graphs(h):
                        last = nc.tensor.transpose(ps_t[h][:, b % HALF, :], xh[:, b, :], ident[:])
                    last.then_inc(xhT_ps, 1)

            def pe_xnT(pe, j):
                for h in range(2):
                    pe.wait_ge(xn_ok, 2 * j + h + 1)
                    if from_octet(j, 2):
                        pe.wait_ge(prT_ok, 2 * j + h - 3)
                    for b in graphs(h):
                        last = nc.tensor.transpose(ps_t[h][:, b % HALF, :], xn[:, b, :], ident[:])
                    last.then_inc(xnT_ps, 1)

            def pe_logits(pe, j):
                for h in range(2):
                    pe.wait_ge(xhT_ok, 2 * j + h + 1)
                    if h == 0 and from_octet(j, 1):
                        pe.wait_ge(rank_read, j)
                    for b in graphs(h):
                        last = nc.tensor.matmul(ps_m[:, 0, b * E:(b + 1) * E], xhT[:, b, :], wrs[:],
                                                start=True, stop=True)
                last.then_inc(lg_ps, 1)

            def pe_front(pe, j, h):
                pe.wait_ge(xnT_ok, 2 * j + h + 1)
                if from_octet(j, 1):
                    pe.wait_ge(u_read, 2 * j + h - 1)
                nc.tensor.matmul(ps_u[h][:], a2rep[:], xnT[:, half(h), :], start=True, stop=False)
                for b in graphs(h):
                    last = nc.tensor.matmul(ps_u[h][:, b % HALF, :], xnT[:, b, :], a1rep[:],
                                            start=False, stop=(b % HALF == HALF - 1))
                last.then_inc(u_ps, 1)
                if h or from_octet(j, 1):
                    pe.wait_ge(wh_ok, 2 * j + h)
                for b in graphs(h):
                    last = nc.tensor.matmul(ps_wh[:, b % HALF, :], xnT[:, b, :], gw[:], start=True, stop=True)
                last.then_inc(wh_ps, 1)

            def pe_prT(pe, j):
                for h in range(2):
                    pe.wait_ge(ex_ok, 2 * j + h + 1)
                    if from_octet(j, 2):
                        pe.wait_ge(xhT_ok, 2 * j + h - 3)
                    for b in graphs(h):
                        last = nc.tensor.transpose(ps_t[h][:, b % HALF, :], ex[:, b, :], ident[:])
                    last.then_inc(prT_ps, 1)

            def pe_attend(pe, j, r):
                for h in range(2):
                    pe.wait_ge(prT_ok, 2 * j + h + 1)
                    pe.wait_ge(wh_ok, 2 * j + h + 1)
                    if from_octet(j, 1):
                        pe.wait_ge(h_read, 2 * j + h - 1)
                    for b in graphs(h):
                        last = nc.tensor.matmul(ps_h[h][:, b % HALF, :], prT[:, b, :], wh[r][:, b, :],
                                                start=True, stop=True)
                    last.then_inc(h_ps, 1)

            def pe_ranks(pe, j):
                pe.wait_ge(both_ok, j + 1)
                rank = ps_m[:, 1, :]
                nc.tensor.matmul(rank, tri[:], both[:], start=True, stop=False)
                for s in range(1, OCT):
                    nc.tensor.matmul(rank[:, s * E:], ones[:], both[:, 0:OCT - s, :], start=False, stop=False)
                nc.tensor.matmul(rank.rearrange("p (b e) -> p b e", e=E), ones[:],
                                 taken[:].unsqueeze(1).to_broadcast([P, OCT, E]),
                                 start=False, stop=True).then_inc(rank_ps, 1)

            def act_xhT(act, j):
                for h in range(2):
                    act.wait_ge(xhT_ps, 2 * j + h + 1)
                    if h == 0 and from_octet(j, 1):
                        act.wait_ge(lg_ps, j)
                    nc.scalar.copy(xhT[:, half(h), :], ps_t[h][:]).then_inc(xhT_ok, 1)

            def act_xnT(act, j):
                for h in range(2):
                    act.wait_ge(xnT_ps, 2 * j + h + 1)
                    if from_octet(j, 1):
                        act.wait_ge(wh_ps, 2 * j + h - 1)
                    nc.scalar.copy(xnT[:, half(h), :], ps_t[h][:]).then_inc(xnT_ok, 1)

            def act_exp(act, j, h):
                act.wait_ge(nbig_ok, j + 1)
                act.wait_ge(e_ok, 2 * j + h + 1)
                for b in graphs(h):
                    last = nc.scalar.activation(ex[:, b, :], ex[:, b, :], ACT.Exp, bias=nbig[:, b:b + 1],
                                                accum_out=den[:, b:b + 1])
                last.then_inc(ex_ok, 1)

            def act_wh(act, j, r, h):
                act.wait_ge(wh_ps, 2 * j + h + 1)
                if from_octet(j, 2):
                    act.wait_ge(h_ps, 2 * j + h - 3)
                nc.scalar.copy(wh[r][:, half(h), :], ps_wh[:]).then_inc(wh_ok, 1)

            def act_prT(act, j):
                for h in range(2):
                    act.wait_ge(prT_ps, 2 * j + h + 1)
                    if from_octet(j, 1):
                        act.wait_ge(h_ps, 2 * j + h - 1)
                    nc.scalar.copy(prT[:, half(h), :], ps_t[h][:]).then_inc(prT_ok, 1)

            def act_stage(act, j, r, turn):
                act.wait_ge(xh_ok, j + 1)
                act.wait_ge(xh2_ok, j + 1)
                if from_octet(j, 2):
                    act.wait_ge(scattered[r], 16 * 2 * OCT * turn)
                for k in range(2):
                    nc.scalar.copy(stage[r][:, k, :, 0:D], xh[:]).then_inc(copied, 1)

            def act_gap(act, j):
                act.wait_ge(gap_ok, j + 1)
                nc.scalar.activation(egap[:], gap[:], ACT.Exp).then_inc(egap_ok, 1)

            def act_norm1(act, j):
                act.wait_ge(root1_ok, 2 * j + 2)
                for h in range(2):
                    if from_octet(j, 1):
                        act.wait_ge(xnT_ps, 2 * j + h - 1)
                    for b in graphs(h):
                        last = nc.scalar.activation(xn[:, b, :], tok[:, ds(j * OCT + b, 1), :].squeeze(1),
                                                    ACT.Identity, bias=shift1[:, b:b + 1], scale=root1[:, b:b + 1])
                    last.then_inc(xn_ok, 1)

            def act_norm2(act, j):
                act.wait_ge(root2_ok, 2 * j + 2)
                if from_octet(j, 1):
                    act.wait_ge(xhT_ps, 2 * j)
                    act.wait_ge(copied, 2 * j)
                for b in graphs(1):
                    last = nc.scalar.activation(xh[:, b, :], tok[:, ds(j * OCT + b, 1), :].squeeze(1), ACT.Identity,
                                                bias=shift2[:, b - HALF:b - HALF + 1],
                                                scale=root2[:, b - HALF:b - HALF + 1])
                last.then_inc(xh2_ok, 1)

            def pool_scatter(pool, j, r):
                wait_apart(pool, slots_ok, j + 1, passed_pool)
                scatter_rows(r)

            class Chain:

                def __init__(self, dve, step):
                    self.dve, self.step, self.n = dve, step, 0
                    dve.sem_clear(step)

                def mark(self, ins):
                    self.n += 1
                    ins.then_inc(self.step, 1)

                def follow(self):
                    self.dve.wait_ge(self.step, self.n)

            def alternate(*streams):
                streams = list(streams)
                while streams:
                    for stream in list(streams):
                        if next(stream, None) is None:
                            streams.remove(stream)

            def dve_scores(dve, j):
                chain = Chain(dve, score_step)
                if from_octet(j, 1):
                    dve.wait_ge(ex_ok, 2 * j)
                    chain.mark(nc.vector.reciprocal(rden[:], den[:]))
                for h in range(2):
                    wait_apart(dve, u_ps, 2 * j + h + 1, passed_dve)
                    for b in graphs(h):
                        last = nc.vector.tensor_tensor_reduce(out=um[:, b, :], in0=ps_u[h][:, b % HALF, :],
                                                              in1=mask[:], scale=1.0, scalar=LOWEST, op0=ALU.add,
                                                              op1=ALU.max, accum_out=top[:, b:b + 1])
                    last.then_inc(u_read, 1)
                dve.wait_ge(u_read, 2 * j + 2)
                chain.mark(nc.vector.tensor_scalar(ntop[:], top[:], -1.0, None, ALU.mult))
                for h in range(2):
                    if from_octet(j, 1):
                        dve.wait_ge(prT_ps, 2 * j + h - 1)
                    nc.vector.scalar_tensor_tensor(ex[:, half(h), :], um[:, half(h), :], SLOPE, um[:, half(h), :],
                                                   ALU.mult, ALU.max).then_inc(e_ok, 1)
                    if h == 0:
                        chain.follow()
                        nc.vector.scalar_tensor_tensor(nbig[:], ntop[:], SLOPE, ntop[:],
                                                       ALU.mult, ALU.min).then_inc(nbig_ok, 1)

            def dve_last_sums(dve, j):
                dve.wait_ge(ex_ok, 2 * j + 2)
                chain = Chain(dve, score_step)
                chain.mark(nc.vector.reciprocal(rden[:], den[:]))
                chain.follow()

            def dve_residual(dve, j):
                for h in range(2):
                    dve.wait_ge(h_ps, 2 * j + h + 1)
                    for b in graphs(h):
                        t = tok[:, ds(j * OCT + b, 1), :].squeeze(1)
                        last = nc.vector.scalar_tensor_tensor(t, ps_h[h][:, b % HALF, :], rden[:, b:b + 1], t,
                                                              ALU.mult, ALU.add)
                    last.then_inc(h_read, 1)

            def dve_moments2(dve, j):
                chain = Chain(dve, moment2_step)
                for h in range(2):
                    wait_apart(dve, h_read, 2 * j + h + 1, passed_dve)
                    for b in graphs(h):
                        chain.mark(nc.vector.bn_stats(bn2[:, b, :], tok[:, ds(j * OCT + b, 1), :]))
                for b in range(OCT):
                    dve.wait_ge(moment2_step, b + 1)
                    last = nc.vector.bn_aggr(mv2[:, b, :], bn2[:, b, :])
                chain.mark(last)

            def dve_moments1(dve, j, r):
                chain = Chain(dve, moment1_step)
                for b in range(OCT):
                    chain.mark(nc.vector.bn_stats(bn[:, b, :], tok[:, ds(j * OCT + b, 1), :]))
                    yield True
                for b in range(OCT):
                    dve.wait_ge(moment1_step, b + 1)
                    last = nc.vector.bn_aggr(mv[r][:, b, :], bn[:, b, :])
                    if b < OCT - 1:
                        yield True
                chain.mark(last)
                yield True
                chain.follow()

            def dve_roots(dve, one, r_one, two):
                chain = Chain(dve, root_step)
                if one is not None:
                    chain.mark(nc.vector.tensor_scalar(var[:, 0, :], mv[r_one][:, :, 1], EPS, None, ALU.add))
                    yield True
                if two is not None:
                    dve.wait_ge(moment2_step, OCT + 1)
                    chain.mark(nc.vector.tensor_scalar(var[:, 1, :], mv2[:, :, 1], EPS, None, ALU.add))
                    yield True
                    chain.follow()
                    chain.mark(nc.vector.scalar_tensor_tensor(var[:, 2, :], var[:, 1, :], EPS, mv2[:, :, 1],
                                                              ALU.mult, ALU.add))
                    yield True
                n = slice(0 if one is not None else 1, 3 if two is not None else 1)
                chain.follow()
                chain.mark(nc.vector.tensor_scalar(seed[:, n, :].bitcast(I32), var[:, n, :].bitcast(I32),
                                                   -0.5, ROOT_SEED, ALU.mult, ALU.add))
                yield True
                src, dst = seed, root
                for _ in range(3):
                    chain.follow()
                    chain.mark(nc.vector.tensor_tensor(tiny[:, n, :], src[:, n, :], src[:, n, :], ALU.mult))
                    yield True
                    chain.follow()
                    chain.mark(nc.vector.scalar_tensor_tensor(tiny[:, n, :], tiny[:, n, :], -0.5, var[:, n, :],
                                                              ALU.mult, ALU.mult))
                    yield True
                    chain.follow()
                    chain.mark(nc.vector.scalar_tensor_tensor(dst[:, n, :], tiny[:, n, :], 1.5, src[:, n, :],
                                                              ALU.add, ALU.mult))
                    yield True
                    src, dst = dst, src
                chain.follow()
                if two is not None:
                    chain.mark(nc.vector.tensor_tensor(tiny[:, 0, :], var[:, 2, :], src[:, 2, :], ALU.mult))
                    yield True
                if one is not None:
                    if from_octet(one, 1):
                        dve.wait_ge(xn_ok, 2 * one)
                    nc.vector.tensor_copy(root1[:], src[:, 0, :]).then_inc(root1_ok, 1)
                    yield True
                    nc.vector.scalar_tensor_tensor(shift1[:], mv[r_one][:, :, 0], -1.0, src[:, 0, :],
                                                   ALU.mult, ALU.mult).then_inc(root1_ok, 1)
                    yield True
                if two is not None:
                    if from_octet(two, 1):
                        dve.wait_ge(xh2_ok, two)
                    nc.vector.tensor_copy(root2[:], src[:, 2, HALF:]).then_inc(root2_ok, 1)
                    yield True
                    nc.vector.scalar_tensor_tensor(shift2[:], mv2[:, HALF:, 0], -1.0, src[:, 2, HALF:],
                                                   ALU.mult, ALU.mult).then_inc(root2_ok, 1)
                    yield True
                    if from_octet(two, 1):
                        dve.wait_ge(lg_read, two)
                    chain.follow()
                    chain.mark(nc.vector.tensor_tensor(ratio[:], tiny[:, 0, :], src[:, 1, :], ALU.mult))
                    yield True
                    chain.follow()

            def dve_norm2(dve, j):
                if from_octet(j, 1):
                    dve.wait_ge(xhT_ps, 2 * j - 1)
                    dve.wait_ge(copied, 2 * j)
                for b in graphs(0):
                    last = nc.vector.tensor_scalar(xh[:, b, :], tok[:, ds(j * OCT + b, 1), :].squeeze(1),
                                                   mv2[:, b, 0:1], root[:, 2, b:b + 1], ALU.subtract, ALU.mult)
                    if b < HALF - 1:
                        yield True
                last.then_inc(xh_ok, 1)
                yield True

            def wide(v):
                return v.unsqueeze(2).to_broadcast([P, OCT, E])

            def each(v):
                return v.unsqueeze(1).to_broadcast([P, OCT, E])

            def dve_choose(dve, j):
                chain = Chain(dve, choice_step)
                dve.wait_ge(lg_ps, j + 1)
                nc.vector.tensor_tensor(lg[:], ps_m[:, 0, :].rearrange("p (b e) -> p b e", e=E), wide(ratio[:]),
                                        ALU.mult).then_inc(lg_read, 1)
                yield True
                dve.wait_ge(lg_read, j + 1)
                chain.mark(nc.vector.tensor_tensor(lg[:], lg[:], each(brs[:]), ALU.add))
                yield True
                for k, src in enumerate((lg, lg2)):
                    chain.follow()
                    chain.mark(nc.vector.tensor_reduce(best[:, k, :], src[:], AX.X, ALU.max))
                    yield True
                    chain.follow()
                    chain.mark(nc.vector.tensor_tensor(eq[:], src[:], wide(best[:, k, :]), ALU.is_equal))
                    yield True
                    chain.follow()
                    chain.mark(nc.vector.tensor_tensor(eq[:], eq[:], each(ranked[:]), ALU.mult))
                    yield True
                    chain.follow()
                    chain.mark(nc.vector.tensor_reduce(pick[:], eq[:], AX.X, ALU.max))
                    yield True
                    chain.follow()
                    chain.mark(nc.vector.tensor_tensor(hot[:, k], wide(pick[:]), each(ranked[:]), ALU.is_equal))
                    yield True
                    chain.follow()
                    if k == 0:
                        chain.mark(nc.vector.scalar_tensor_tensor(lg2[:], hot[:, 0], LOWEST, lg[:],
                                                                  ALU.mult, ALU.add))
                        yield True
                nc.vector.tensor_tensor(both[:], hot[:, 0], hot[:, 1], ALU.add).then_inc(both_ok, 1)
                yield True
                nc.vector.tensor_tensor(gap[:], best[:, 1, :], best[:, 0, :], ALU.subtract).then_inc(gap_ok, 1)
                yield True

            def dve_place(dve, j, r):
                chain = Chain(dve, place_step)
                dve.wait_ge(copied, 2 * j + 2)
                chain.mark(nc.vector.tensor_copy(stage[r][:, :, :, D].bitcast(I32),
                                                 ids[:, ds(j * OCT, OCT)].unsqueeze(1).to_broadcast([P, 2, OCT])))
                yield True
                dve.wait_ge(egap_ok, j + 1)
                chain.mark(nc.vector.tensor_scalar(share[:], egap[:], 1.0, None, ALU.add))
                yield True
                chain.follow()
                chain.mark(nc.vector.reciprocal(stage[r][:, 0, :, D + 1], share[:]))
                yield True
                chain.follow()
                chain.mark(nc.vector.tensor_tensor(stage[r][:, 1, :, D + 1], egap[:], stage[r][:, 0, :, D + 1],
                                                   ALU.mult))
                yield True
                dve.wait_ge(rank_ps, j + 1)
                nc.vector.tensor_tensor(place[:], ps_m[:, 1, :].rearrange("p (b e) -> p b e", e=E),
                                        each(region[:]), ALU.add).then_inc(rank_read, 1)
                yield True
                dve.wait_ge(rank_read, j + 1)
                chain.mark(nc.vector.tensor_tensor(
                    chosen[:].rearrange("p k b e -> p k (b e)"), hot[:].rearrange("p k b e -> p k (b e)"),
                    place[:].rearrange("p b e -> p (b e)").unsqueeze(1).to_broadcast([P, 2, OCT * E]), ALU.mult))
                yield True
                chain.mark(nc.vector.tensor_reduce(new[:], both[:].rearrange("p b e -> p e b"), AX.X, ALU.add))
                chain.follow()
                with nc.allow_low_precision(reason="one term of each sum is not zero, a whole number below 2^24"):
                    nc.vector.tensor_reduce(slots[r][:], chosen[:], AX.X, ALU.add).then_inc(slots_ok, 1)
                yield True
                chain.mark(nc.vector.tensor_tensor(taken[:], taken[:], new[:], ALU.add))
                yield True
                chain.follow()

            def dve_plan(dve):
                chain = Chain(dve, plan_step)

                def link(ins):
                    chain.mark(ins)
                    chain.follow()

                dve.wait_ge(count_ps, 1)
                link(nc.vector.tensor_copy(count[:].rearrange("o k e -> o (k e)"), ps_m[0:1, 0, 0:2 * E]))
                nc.vector.tensor_tensor(tails[:], count[:, 0, :], region[0:1, :], ALU.add).then_inc(tails_ok, 1)
                link(nc.vector.tensor_tensor(fills, count[:, 0, :].unsqueeze(2).to_broadcast([1, E, KT]),
                                             kth[:].unsqueeze(1).to_broadcast([1, E, KT]), ALU.is_gt))
                link(nc.vector.tensor_reduce(tiles[:], fills, AX.X, ALU.add))
                link(nc.vector.tensor_copy(ends[:, 0:1], tiles[:, 0:1]))
                for e in range(1, E):
                    link(nc.vector.tensor_tensor(ends[:, e:e + 1], ends[:, e - 1:e], tiles[:, e:e + 1], ALU.add))
                link(nc.vector.tensor_tensor(past, jth[:].unsqueeze(2).to_broadcast([1, NE, E]),
                                             ends[:].unsqueeze(1).to_broadcast([1, NE, E]), ALU.is_ge))
                link(nc.vector.tensor_reduce(who[:], past, AX.X, ALU.add))
                link(nc.vector.tensor_tensor(past, past, tiles[:].unsqueeze(1).to_broadcast([1, NE, E]),
                                             ALU.mult))
                link(nc.vector.tensor_reduce(before[:], past, AX.X, ALU.add))
                link(nc.vector.tensor_tensor(rowf[:], jth[:], before[:], ALU.subtract))
                link(nc.vector.tensor_scalar(live[:], who[:], float(E), None, ALU.is_lt))
                link(nc.vector.tensor_tensor(rowf[:], rowf[:], live[:], ALU.mult))
                link(nc.vector.tensor_scalar(live[:], who[:], float(E), None, ALU.is_ge))
                link(nc.vector.tensor_tensor(live[:], live[:], odd[:, 0:NE], ALU.mult))
                link(nc.vector.tensor_tensor(rowf[:], rowf[:], live[:], ALU.add))
                link(nc.vector.tensor_scalar(rowf[:], rowf[:], float(TILE), None, ALU.mult))
                nc.vector.scalar_tensor_tensor(table[:, 0, :], who[:], float(CAP), rowf[:],
                                               ALU.mult, ALU.add).then_inc(table_ok, 1)
                dve.wait_ge(table_ok, 1)
                link(nc.vector.tensor_scalar(reach[:], who[:, 0:FIRST], -1.0, float(E), ALU.mult, ALU.add))
                link(nc.vector.tensor_tensor(sooner[:], ranked[0:1, :].unsqueeze(1).to_broadcast([1, FIRST, E]),
                                             reach[:].unsqueeze(2).to_broadcast([1, FIRST, E]), ALU.is_equal))
                link(nc.vector.tensor_tensor(sooner[:], sooner[:],
                                             count[:, 1, :].unsqueeze(1).to_broadcast([1, FIRST, E]), ALU.mult))
                link(nc.vector.tensor_reduce(reach[:], sooner[:], AX.X, ALU.add))
                link(nc.vector.scalar_tensor_tensor(reach[:], rowf[:, 0:FIRST], float(TILE), reach[:],
                                                    ALU.add, ALU.is_le))
                nc.vector.tensor_scalar(table[:, 6, 0:FIRST], reach[:], -16.0 * 2 * OCT, 16.0 * OCT * NO,
                                        ALU.mult, ALU.add).then_inc(table_ok, 1)
                link(nc.vector.tensor_scalar(who[:], who[:], float(E - 1), None, ALU.min))
                nc.vector.tensor_copy(table[:, 1, :], who[:]).then_inc(table_ok, 1)
                nc.vector.tensor_scalar(table[:, 2, :], who[:], float(HC + 1), None, ALU.mult).then_inc(table_ok, 1)
                nc.vector.tensor_tensor(table[:, 5, 2:NE], who[:, 2:NE], who[:, 0:NE - 2],
                                        ALU.not_equal).then_inc(table_ok, 1)
                link(nc.vector.tensor_scalar(pairs[:], before[:], 0.5, -0.25, ALU.mult, ALU.add))
                link(nc.vector.tensor_scalar(pairs[:], pairs[:], WHOLE, None, ALU.add))
                link(nc.vector.tensor_scalar(pairs[:], pairs[:], WHOLE, None, ALU.subtract))
                link(nc.vector.tensor_tensor(before[:], before[:], pairs[:], ALU.subtract))
                nc.vector.tensor_scalar(table[:, 3, :], before[:], 1.0, 16.0 * CH, ALU.max, ALU.mult).then_inc(table_ok, 1)
                nc.vector.tensor_scalar(table[:, 4, :], pairs[:], 1.0, 16.0 * CH, ALU.max, ALU.mult).then_inc(table_ok, 1)
                dve.wait_ge(table_ok, 7)


            def pe_bias(pe):
                pe.wait_ge(vecs_in, 64)
                pe.wait_ge(u_read, 2 * NO)
                nc.tensor.transpose(ps_u[0][:].rearrange("p b n -> p (b n)")[:, 0:NV], vecs[:],
                                    ident[0:NV, 0:NV]).then_inc(cols_ps, 1)
                pe.wait_ge(all_taken, 1)
                nc.tensor.matmul(ps_m[:, 0, 0:E], ones[:], taken[:], start=True, stop=True)
                nc.tensor.matmul(ps_m[:, 0, E:2 * E], ones[:], early[:], start=True, stop=True).then_inc(count_ps, 1)
                pe.wait_ge(cols_ok, 1)
                pe.wait_ge(wh_ok, 2 * NO)
                for e in range(E):
                    pe.wait_ge(raw1_in[e // 2], 16)
                    for c in range(HC):
                        mm = nc.tensor.matmul(ps_wh[:, 0, e * HC + c:e * HC + c + 1], raw1[:, e, c * P:(c + 1) * P],
                                              cols[:, LB + e:LB + e + 1], start=True, stop=True)
                    mm.then_inc(b1_ps, 1)

            def act_weights2(act, experts):
                for e in experts:
                    act.wait_ge(raw2_in[e // 2], 32)
                    nc.scalar.activation(w2s[:, e, 0, :], raw2[:, e, :], ACT.Copy).then_inc(high2, 1)

            def act_weights1(act):
                act.wait_ge(cols_ok, 1)
                for e in range(E):
                    act.wait_ge(raw1_in[e // 2], 16)
                    nc.scalar.activation(w1s[:, e, 0, :], raw1[:, e, :], ACT.Copy,
                                         scale=cols[:, LG + e:LG + e + 1]).then_inc(high1, 1)

            def dve_columns(dve):
                dve.wait_ge(cols_ps, 1)
                nc.vector.tensor_copy(cols[:], ps_u[0][:].rearrange("p b n -> p (b n)")[:, 0:NV]).then_inc(cols_ok, 1)
                dve.wait_ge(cols_ok, 1)
                nc.vector.tensor_copy(bias[:, :, HC:HC + 1], cols[:, B2:LG].unsqueeze(2)).then_inc(bias_ok, 1)

            def dve_weights2(dve, experts):
                for e in experts:
                    dve.wait_ge(high2, e + 1)
                    nc.vector.tensor_tensor(w2s[:, e, 1, :], raw2[:, e, :], w2s[:, e, 0, :].bitcast(F32),
                                            ALU.subtract).then_inc(low2, 1)

            def dve_weights1(dve):
                for e in range(E):
                    dve.wait_ge(high1, e + 1)
                    dve.wait_ge(b1_ps, e + 1)
                    nc.vector.scalar_tensor_tensor(w1s[:, e, 1, :], raw1[:, e, :], cols[:, LG + e:LG + e + 1],
                                                   w1s[:, e, 0, :].bitcast(F32), ALU.mult,
                                                   ALU.subtract).then_inc(low1, 1)
                dve.wait_ge(b1_ps, E)
                nc.vector.tensor_tensor(bias[:, :, 0:HC],
                                        ps_wh[:, 0, 0:E * HC].rearrange("p (e c) -> p e c", c=HC),
                                        cols[:, 0:B2].rearrange("p (e c) -> p e c", c=HC),
                                        ALU.add).then_inc(bias_ok, 1)
                dve.wait_ge(bias_ok, 2)

            half_of_experts = (range(0, E // 2), range(E // 2, E))


            def has(j):
                return not isinstance(j, int) or 0 <= j < NO

            def pe_iteration(pe, i, r):
                if has(i - 1):
                    pe_attend(pe, i - 1, 1 - r)
                if has(i + 1):
                    pe_xnT(pe, i + 1)
                if has(i - 2):
                    pe_xhT(pe, i - 2)
                if has(i + 1):
                    pe_front(pe, i + 1, 0)
                if has(i - 2):
                    pe_logits(pe, i - 2)
                if has(i + 1):
                    pe_front(pe, i + 1, 1)
                if has(i):
                    pe_prT(pe, i)
                if has(i - 2):
                    pe_ranks(pe, i - 2)

            def act_iteration(act, i, r, turn):
                if has(i + 1):
                    act_xnT(act, i + 1)
                if has(i - 2):
                    act_xhT(act, i - 2)
                if has(i):
                    act_exp(act, i, 0)
                if has(i):
                    act_exp(act, i, 1)
                if has(i - 2):
                    act_stage(act, i - 2, r, turn)
                if has(i + 1):
                    act_wh(act, i + 1, 1 - r, 0)
                if has(i + 1):
                    act_wh(act, i + 1, 1 - r, 1)
                if has(i):
                    act_prT(act, i)
                if has(i - 2):
                    act_gap(act, i - 2)
                if has(i + 2):
                    act_norm1(act, i + 2)
                if has(i - 1):
                    act_norm2(act, i - 1)
                if isinstance(i, int) and i in (NO - 1, NO):
                    act_weights2(act, half_of_experts[i - NO + 1])

            def dve_iteration(dve, i, r):
                if has(i):
                    dve_scores(dve, i)
                elif has(i - 1):
                    dve_last_sums(dve, i - 1)
                if has(i - 1):
                    dve_residual(dve, i - 1)
                    dve_moments2(dve, i - 1)
                if isinstance(i, int) and i < HEAD and i + 3 in first_of_part:
                    dve.wait_ge(tok_in[first_of_part.index(i + 3)], 16)
                if isinstance(i, int) and i in (NO, NO + 1):
                    dve_weights2(dve, half_of_experts[i - NO])
                streams = []
                if has(i + 3):
                    streams.append(dve_moments1(dve, i + 3, 1 - r))
                if has(i + 2) or has(i - 1):
                    streams.append(dve_roots(dve, i + 2 if has(i + 2) else None, r, i - 1 if has(i - 1) else None))
                if has(i - 2):
                    streams.append(dve_choose(dve, i - 2))
                alternate(*streams)
                streams = []
                if has(i - 1):
                    streams.append(dve_norm2(dve, i - 1))
                if has(i - 2):
                    streams.append(dve_place(dve, i - 2, r))
                alternate(*streams)

            acc_tokens = acc_dram[0:TOKENS, :].rearrange("(g p) d -> p g d", p=P)
            HEAD, TURNS = 4, (NO - 7) // 2
            REST = HEAD + 2 * TURNS

            def iterations(engine, iteration, before_loop=None):
                for i in range(-3, HEAD):
                    iteration(i, i % 2, (i - 2) // 2)
                if before_loop is not None:
                    before_loop()
                with engine.Fori(0, TURNS) as n:
                    for r in range(2):
                        iteration(2 * n + (HEAD + r), r, n + (HEAD - 2) // 2)
                for i in range(REST, NO + 2):
                    iteration(i, i % 2, (i - 2) // 2)

            with nc.Block() as block:
                @block.sync
                def _(sp):
                    def load_x(n):
                        sp.dma_start(tok[:, parts[n]:parts[n + 1], :],
                                     x[parts[n]:parts[n + 1]].rearrange("g p d -> p g d")).then_inc(tok_in[n], 16)

                    load_x(1)
                    load_x(2)
                    sp.wait_ge(pads_out, 48)
                    load_x(3)
                    sp.dma_start(vecs[0:B2, :], b1.rearrange("e (c p) -> (e c) p", p=P)).then_inc(vecs_in, 16)
                    sp.dma_start(vecs[B2:LG, :], b2).then_inc(vecs_in, 16)
                    sp.dma_start(vecs[LG:LB, :], ln_g).then_inc(vecs_in, 16)
                    sp.dma_start(vecs[LB:NV, :], ln_b).then_inc(vecs_in, 16)
                    for n in range(E // 2):
                        e = slice(2 * n, 2 * n + 2)
                        sp.dma_start(raw1[:, e, :], w1[e].rearrange("e d h -> d e h")).then_inc(raw1_in[n], 16)
                    for e in range(E):
                        sp.dma_start(raw2[:, e, :].rearrange("p (c d) -> p c d", d=D),
                                     w2[e].rearrange("(c p) d -> p c d", p=P)).then_inc(raw2_in[e // 2], 16)

                    def store(i, r, turn):
                        if has(i - 1):
                            sp.wait_ge(h_read, 2 * (i - 1) + 2)
                            sp.dma_start(acc_tokens[:, ds((i - 1) * OCT, OCT), :],
                                         tok[:, ds((i - 1) * OCT, OCT), :]).then_inc(stored, 16)
                    iterations(sp, store)
                    sp.wait_ge(tails_ok, 1)
                    for e in range(E):
                        row = sp.value_load(tails[0:1, e:e + 1], min_val=e * CAP, max_val=e * CAP + TOKENS)
                        sp.dma_start(rows_dram[bass.ds(row, TILE), :], pads_dram).then_inc(padded, 16)
                    sp.wait_ge(table_ok, 7)
                    sp.wait_ge(low2, E)
                    sp.wait_ge(low1, E)
                    for t in range(2):
                        e = sp.value_load(table[0:1, 1, t:t + 1], min_val=0, max_val=E - 1)
                        load_weights(sp, e, t, w1c, w1all, 2 * H, w1_in)
                        if t == 0:
                            load_weights(sp, e, t, w2c, w2all, 2 * HC * D, w2_in)
                    sp.wait_ge(padded, 16 * E)
                    sp.wait_ge(stored, 16 * NO)

                @block.tensor
                def _(pe):
                    iterations(pe, lambda i, r, turn: pe_iteration(pe, i, r))
                    pe_bias(pe)

                @block.scalar
                def _(act):
                    iterations(act, lambda i, r, turn: act_iteration(act, i, r, turn))
                    act_weights1(act)

                @block.gpsimd
                def _(pool):
                    def step_of(i, r, turn):
                        if has(i - 2) and not (isinstance(i, int) and i - 2 == NO - 1):
                            pool_scatter(pool, i - 2, r)
                    iterations(pool, step_of)

                @block.vector
                def _(dve):
                    iterations(dve, lambda i, r, turn: dve_iteration(dve, i, r), lambda: dve.wait_ge(tok_in[3], 16))
                    nc.vector.tensor_tensor(early[:], taken[:], new[:], ALU.subtract).then_inc(all_taken, 1)
                    dve_columns(dve)
                    dve_plan(dve)
                    dve_weights1(dve)

        to_route.close()

        with ExitStack() as ctx:
            def sb(name, shape, dt=F32):
                return ctx.enter_context(nc.sbuf_tensor(name, shape, dt))

            def ps(name, shape):
                return ctx.enter_context(nc.psum_tensor(name, shape, F32))

            def sem(name):
                return ctx.enter_context(nc.semaphore(name))

            XB = 2
            xs = [sb(f"xs{n}", [P, CH, R]) for n in range(XB)]
            w2c.append(sb("w2c1", [P, 2, HC * D], F32R))
            xT = [sb(f"xT{r}", [P, 2, TILE], F32R) for r in range(2)]
            hf = [sb(f"hf{c}", [P, TILE]) for c in range(HC)]
            hs = [sb(f"hs{r}", [P, 2, HC, TILE], F32R) for r in range(2)]
            gelu_try = sb("gelu_try", [P, 1])
            yT = sb("yT", [P, TILE])
            ys = [sb(f"ys{r}", [P, CH, D]) for r in range(2)]
            yid = [sb(f"yid{r}", [P, CH], I32) for r in range(2)]
            tile_id = [sb(f"tile_id{n}", [P, CH], I32) for n in range(4)]
            tile_wt = [sb(f"tile_wt{n}", [P, CH]) for n in range(4)]
            ps_x = ps("ps_x", [P, CH, P])
            ps_l1 = [ps(f"ps_l1_{c}", [P, TILE]) for c in range(HC)]
            ps_l2 = ps("ps_l2", [P, TILE])
            ps_y = ps("ps_y", [P, CH, D])

            x_in = [sem(f"x_in{r}") for r in range(XB)]
            x_ps = sem("x_ps")
            xhigh_ok = sem("xhigh_ok")
            xlow_ok = sem("xlow_ok")
            l1_ps = sem("l1_ps")
            gelu_ok = sem("gelu_ok")
            high_ok = sem("high_ok")
            acthigh_ok = sem("acthigh_ok")
            low_ok = sem("low_ok")
            l2_ps = sem("l2_ps")
            yT_ok = sem("yT_ok")
            y_ps = sem("y_ps")
            ys_ok = sem("ys_ok")
            tail_kept = sem("tail_kept")
            yid_ok = sem("yid_ok")
            passed = sem("passed")
            sent = [sem(f"sent{r}") for r in range(2)]
            out_ok = sem("out_ok")


            def pe_x(pe, t, q, turn):
                pe.wait_ge(x_in[q % 2], 32 * turn + 16 * (q // 2) + 16)
                if not isinstance(t, int) or t >= 1:
                    pe.wait_ge(xlow_ok, t)
                for c in range(CH):
                    last = nc.tensor.transpose(ps_x[:, c, :], xs[q % 2][:, c, 0:D], ident[:])
                last.then_inc(x_ps, 1)

            def pe_layer1(pe, t, q, turn, c):
                r = q % 2
                if c == 0:
                    pe.wait_ge(w1_in[r], 32 * turn + 16 * (q // 2) + 16)
                    pe.wait_ge(xlow_ok, t + 1)
                if not isinstance(t, int) or t >= 1:
                    pe.wait_ge(gelu_ok, HC * t + c - HC + 1)
                for n, (a, b) in enumerate(((0, 0), (0, 1), (1, 0))):
                    last = nc.tensor.matmul(ps_l1[c][:], w1c[r][:, a, c * P:(c + 1) * P], xT[r][:, b, :],
                                            start=(n == 0), stop=(n == 2))
                last.then_inc(l1_ps, 1)

            def pe_layer2(pe, t, q, turn):
                r = q % 2
                pe.wait_ge(w2_in[r], 32 * turn + 16 * (q // 2) + 16)
                if not isinstance(t, int) or t >= 1:
                    pe.wait_ge(yT_ok, t)
                for c in range(HC):
                    pe.wait_ge(low_ok, HC * t + c + 1)
                    for n, (a, b) in enumerate(((0, 0), (0, 1), (1, 0))):
                        last = nc.tensor.matmul(ps_l2[:], w2c[r][:, a, c * D:(c + 1) * D], hs[r][:, b, c, :],
                                                start=(c == 0 and n == 0), stop=(c == HC - 1 and n == 2))
                last.then_inc(l2_ps, 1)

            def pe_y(pe, t):
                pe.wait_ge(yT_ok, t + 1)
                if not isinstance(t, int) or t >= 1:
                    pe.wait_ge(ys_ok, t)
                for c in range(CH):
                    last = nc.tensor.transpose(ps_y[:, c, :], yT[:, c * P:(c + 1) * P], ident[:])
                last.then_inc(y_ps, 1)

            def act_x(act, t, q):
                act.wait_ge(x_ps, t + 1)
                if not isinstance(t, int) or t >= 2:
                    act.wait_ge(l1_ps, HC * t - HC)
                nc.scalar.copy(xT[q % 2][:, 0, :], ps_x[:].rearrange("p c n -> p (c n)")).then_inc(xhigh_ok, 1)

            def act_gelu(act, t, c, column):
                act.wait_ge(l1_ps, HC * t + c + 1)
                if not isinstance(t, int) or t >= 1:
                    act.wait_ge(low_ok, HC * t + c - HC + 1)
                nc.scalar.activation(hf[c][:], ps_l1[c][:], ACT.Gelu,
                                     bias=biases[:, ds(column + c, 1)]).then_inc(gelu_ok, 1)

            def act_high(act, t, q, c):
                act.wait_ge(gelu_ok, HC * t + c + 1)
                if not isinstance(t, int) or t >= 2:
                    act.wait_ge(l2_ps, t - 1)
                nc.scalar.copy(hs[q % 2][:, 0, c, :], hf[c][:]).then_inc(acthigh_ok, 1)

            def act_y(act, t, column):
                act.wait_ge(l2_ps, t + 1)
                if not isinstance(t, int) or t >= 1:
                    act.wait_ge(y_ps, t)
                nc.scalar.activation(yT[:], ps_l2[:], ACT.Identity,
                                     bias=biases[:, ds(column + HC, 1)]).then_inc(yT_ok, 1)

            def dve_x(dve, t, q, turn):
                dve.wait_ge(x_in[q % 2], 32 * turn + 16 * (q // 2) + 16)
                if not isinstance(t, int) or t >= 4:
                    dve.wait_ge(ys_ok, t - 3)
                nc.vector.tensor_copy(tile_id[q][:], xs[q % 2][:, :, D].bitcast(I32)).then_inc(tail_kept, 1)
                nc.vector.tensor_copy(tile_wt[q][:], xs[q % 2][:, :, D + 1]).then_inc(tail_kept, 1)
                dve.wait_ge(xhigh_ok, t + 1)
                if not isinstance(t, int) or t >= 2:
                    dve.wait_ge(l1_ps, HC * t - HC)
                nc.vector.tensor_tensor(xT[q % 2][:, 1, :], ps_x[:].rearrange("p c n -> p (c n)"),
                                        xT[q % 2][:, 0, :].bitcast(F32), ALU.subtract).then_inc(xlow_ok, 1)

            def dve_high(dve, t, q, c):
                dve.wait_ge(gelu_ok, HC * t + c + 1)
                if not isinstance(t, int) or t >= 2:
                    dve.wait_ge(l2_ps, t - 1)
                nc.vector.tensor_copy(hs[q % 2][:, 0, c, :], hf[c][:]).then_inc(high_ok, 1)

            def dve_low(dve, t, q, c):
                if c % 2:
                    dve.wait_ge(acthigh_ok, HC // 2 * t + c // 2 + 1)
                else:
                    dve.wait_ge(high_ok, HC // 2 * t + c // 2 + 1)
                nc.vector.tensor_tensor(hs[q % 2][:, 1, c, :], hf[c][:], hs[q % 2][:, 0, c, :].bitcast(F32),
                                        ALU.subtract).then_inc(low_ok, 1)

            def dve_y(dve, t, q, turn):
                r = q % 2
                dve.wait_ge(y_ps, t + 1)
                if not isinstance(t, int) or t >= 2:
                    dve.wait_ge(sent[r], 16 * CH * 2 * turn + 16 * CH * (q // 2))
                dve.wait_ge(tail_kept, 2 * t + 2)
                nc.vector.tensor_copy(yid[r][:], tile_id[q][:]).then_inc(yid_ok, 1)
                nc.vector.tensor_tensor(ys[r][:], ps_y[:], tile_wt[q][:].unsqueeze(2).to_broadcast([P, CH, D]),
                                        ALU.mult).then_inc(ys_ok, 1)

            def pool_y(pool, t, q):
                wait_apart(pool, ys_ok, t + 1, passed)
                wait_apart(pool, yid_ok, t + 1, passed)
                for parity in range(2):
                    if not isinstance(t, int) or t >= 1 + parity:
                        need = pool.value_load(table[0:1, 3 + parity, ds(t, 1)], min_val=1, max_val=16 * CH * NT)
                        wait_apart(pool, sent[parity], need, passed)
                for c in range(CH):
                    nc.gpsimd.indirect_dma_start(
                        out=acc_dram, out_offset=bass.IndirectOffsetOnAxis(ap=yid[q % 2][:, c:c + 1], axis=0),
                        in_=ys[q % 2][:, c, :], in_offset=None,
                        compute_op=ALU.add).then_inc(sent[q % 2], 16)

            def sp_x(sp, t, q):
                row = sp.value_load(table[0:1, 0, ds(t, 1)], min_val=0, max_val=E * CAP + TILE)
                if isinstance(t, int) and t < FIRST:
                    wait_apart(sp, scattered[1], sp.value_load(table[0:1, 6, t:t + 1], min_val=1,
                                                               max_val=16 * OCT * NO), passed)
                elif isinstance(t, int) and t == FIRST:
                    sp.wait_ge(scattered[1], 16 * OCT * NO)
                if not isinstance(t, int) or t >= XB:
                    sp.wait_ge(x_ps, t - XB + 1)
                    sp.wait_ge(tail_kept, 2 * (t - XB) + 2)
                sp.dma_start(xs[q % 2][:], rows_dram[bass.ds(row, TILE), :].rearrange("(c p) r -> p c r", p=P)
                             ).then_inc(x_in[q % 2], 16)

            def sp_weights(sp, t, q, read, count, buffers, source, width, arrived):
                e = sp.value_load(table[0:1, 1, ds(t, 1)], min_val=0, max_val=E - 1)
                other = sp.value_load(table[0:1, 5, ds(t, 1)], min_val=0, max_val=1)
                wait_apart(sp, read, count, passed)
                with sp.If(other == 1):
                    load_weights(sp, e, q % 2, buffers, source, width, arrived)
                with sp.If(other == 0):
                    sp.sem_inc(arrived[q % 2], 16)

            def sp_w1(sp, t, q):
                sp_weights(sp, t, q, l1_ps, HC * t - HC, w1c, w1all, 2 * H, w1_in)

            def sp_w2(sp, t, q):
                sp_weights(sp, t, q, l2_ps, t - 1, w2c, w2all, 2 * HC * D, w2_in)

            biases = bias[:].rearrange("p e c -> p (e c)")

            HEAD = 4
            LOOPS = (NT - HEAD - 1) // 4
            REST = HEAD + 4 * LOOPS

            def previous(q, turn, n):
                return (q - n) % 4, turn + (q - n) // 4

            def iterations(engine, step_of):
                for t in range(HEAD):
                    step_of(t, t % 4, t // 4)
                with engine.Fori(0, LOOPS) as n:
                    for k in range(4):
                        step_of(4 * n + (HEAD + k), (HEAD + k) % 4, n + (HEAD + k) // 4)
                for t in range(REST, NT + 2):
                    step_of(t, t % 4, t // 4)

            def present(t, low, high=NT):
                return not isinstance(t, int) or low <= t < high

            with nc.Block() as block:
                @block.gpsimd
                def _(pool):
                    def step_of(t, q, turn):
                        if present(t, 2, NT + 2):
                            pool_y(pool, t - 2, (q - 2) % 4)
                    scatter_rows((NO - 1) % 2)
                    iterations(pool, step_of)
                    for r in range(2):
                        pool.wait_ge(sent[r], 16 * CH * ((NT - r + 1) // 2))

                @block.sync
                def _(sp):
                    sp.wait_ge(scattered[0], 16 * OCT * NO)
                    sp_x(sp, 0, 0)
                    sp_x(sp, 1, 1)
                    e = sp.value_load(table[0:1, 1, 1:2], min_val=0, max_val=E - 1)
                    load_weights(sp, e, 1, w2c, w2all, 2 * HC * D, w2_in)

                    def step_of(t, q, turn):
                        if present(t, 0, NT - 2):
                            sp_x(sp, t + 2, (q + 2) % 4)
                            sp_w1(sp, t + 2, (q + 2) % 4)
                        if present(t, 1, NT - 1):
                            sp_w2(sp, t + 1, (q + 1) % 4)
                    iterations(sp, step_of)
                    for parity in range(2):
                        wait_apart(sp, sent[parity], sp.value_load(table[0:1, 3 + parity, NT:NE], min_val=1,
                                                                   max_val=16 * CH * NT), passed)
                    for o in range(0, G, OCT):
                        sp.dma_start(out[o:o + OCT].rearrange("g p d -> (g p) d"),
                                     acc_dram[o * N:(o + OCT) * N, :]).then_inc(out_ok, 16)
                    sp.wait_ge(out_ok, 16 * NO)

                @block.tensor
                def _(pe):
                    pe_x(pe, 0, 0, 0)

                    def step_of(t, q, turn):
                        if present(t, 0):
                            pe_layer1(pe, t, q, turn, 0)
                            pe_layer1(pe, t, q, turn, 1)
                        if present(t, 0, NT - 1):
                            pe_x(pe, t + 1, (q + 1) % 4, turn + (q + 1) // 4)
                        if present(t, 0):
                            pe_layer1(pe, t, q, turn, 2)
                            pe_layer1(pe, t, q, turn, 3)
                        if present(t, 2, NT + 2):
                            pe_y(pe, t - 2)
                        if present(t, 1, NT + 1):
                            pe_layer2(pe, t - 1, *previous(q, turn, 1))
                    iterations(pe, step_of)

                @block.scalar
                def _(act):
                    nc.scalar.activation(gelu_try[:], ident[:, 0:1], ACT.Gelu)
                    act_x(act, 0, 0)

                    def step_of(t, q, turn):
                        if present(t, 2, NT + 2):
                            column = act.value_load(table[0:1, 2, ds(t - 2, 1)], min_val=0, max_val=(E - 1) * (HC + 1))
                            act_y(act, t - 2, column)
                        if present(t, 0):
                            column = act.value_load(table[0:1, 2, ds(t, 1)], min_val=0, max_val=(E - 1) * (HC + 1))
                            act_gelu(act, t, 0, column)
                            act_gelu(act, t, 1, column)
                            act_high(act, t, q, 1)
                        if present(t, 0, NT - 1):
                            act_x(act, t + 1, (q + 1) % 4)
                        if present(t, 0):
                            act_gelu(act, t, 2, column)
                            act_gelu(act, t, 3, column)
                            act_high(act, t, q, 3)
                    iterations(act, step_of)

                @block.vector
                def _(dve):
                    dve_x(dve, 0, 0, 0)

                    def step_of(t, q, turn):
                        if present(t, 0):
                            dve_high(dve, t, q, 0)
                            dve_low(dve, t, q, 0)
                            dve_low(dve, t, q, 1)
                        if present(t, 0, NT - 1):
                            dve_x(dve, t + 1, (q + 1) % 4, turn + (q + 1) // 4)
                        if present(t, 0):
                            dve_high(dve, t, q, 2)
                            dve_low(dve, t, q, 2)
                        if present(t, 2, NT + 2):
                            dve_y(dve, t - 2, *previous(q, turn, 2))
                        if present(t, 0):
                            dve_low(dve, t, q, 3)
                    iterations(dve, step_of)


_INS = ["x", "adj", "L0_gnn_W", "L0_gnn_a", "L0_ffn_Wr", "L0_ffn_br", "L0_ffn_ln_g", "L0_ffn_ln_b",
        "L0_ffn_W1", "L0_ffn_b1", "L0_ffn_W2", "L0_ffn_b2"]


def kernel(**inputs):
    import numpy as np
    import concourse.bacc as bacc
    from concourse.bass_utils import run_bass_kernel_spmd

    nc = bacc.Bacc("TRN2", target_bir_lowering=False, num_devices=1)
    arrays, args = {}, []
    for name in _INS:
        a = np.ascontiguousarray(inputs[name])
        arrays[f"in_{name}"] = a
        args.append(nc.dram_tensor(f"in_{name}", a.shape, mybir.dt.from_np(a.dtype), kind="ExternalInput").ap())
    shape = inputs["x"].shape
    out = nc.dram_tensor("out_0", shape, F32, kind="ExternalOutput").ap()
    moe_kernel(nc, *args, out)
    r = run_bass_kernel_spmd(nc, [arrays], core_ids=[0])
    return r.results[0]["out_0"]
```
